# Optimizing a Trainium2 kernel written in Bass

```python
import numpy as np
import jax
import jax.numpy as jnp

def _softmax(x, axis=-1):
    return jax.nn.softmax(x, axis=axis)

def _gelu(x):
    return jax.nn.gelu(x, approximate=True)

def _silu(x):
    return jax.nn.silu(x)

def _sigmoid(x):
    return jax.nn.sigmoid(x)

def _layernorm(x, axis=-1, eps=1e-05):
    m = jnp.mean(x, axis=axis, keepdims=True)
    v = jnp.var(x, axis=axis, keepdims=True)
    return (x - m) / jnp.sqrt(v + eps)

def _scatter_add(tgt, idx, src, axis=0):
    return tgt.at[idx].add(src)

def _segment_sum(src, seg, n):
    return jax.ops.segment_sum(src, seg, n)
kernel_name = 'mk_decoder_preln_d1_seqx_r4_4c4cb6'

def setup_inputs(seed: int=0):
    np.random.seed(seed)
    _w = jnp.asarray

    def _rec_inputs():
        import jax
        import jax.numpy as jnp
        _rk = jax.random.key(seed)
        x = -0.000125 + 0.9999 * jax.random.normal(jax.random.fold_in(_rk, 1), (4, 512, 512), jnp.float32)
        _lenS = 512 - jax.random.randint(jax.random.fold_in(_rk, 7), (4,), 0, max(1, 512 // 4) + 1, jnp.int32)
        _lenS2 = 64 - jax.random.randint(jax.random.fold_in(_rk, 8), (4,), 0, max(1, 64 // 4) + 1, jnp.int32)
        _ctx_2048P = jax.random.normal(jax.random.fold_in(_rk, 11), (4, 16, 512), jnp.float32)
        _ctx_2048c = jax.random.dirichlet(jax.random.fold_in(_rk, 511), 0.3 * jnp.ones((16,), jnp.float32), (4, 64))
        _ctx_2048t = jnp.einsum('bsk,bkd->bsd', _ctx_2048c, _ctx_2048P)
        _ctx_2048t = _ctx_2048t * jax.lax.rsqrt(jnp.mean(jnp.square(_ctx_2048t)) + 1e-12) * 0.953939
        ctx_2048 = 0.00222621 + 0.99962 * (_ctx_2048t + 0.3 * jax.random.normal(jax.random.fold_in(_rk, 611), (4, 64, 512), jnp.float32))
        itok_Sx4_0_63 = jax.random.randint(jax.random.fold_in(_rk, 12), (512, 4), 0, 64, jnp.int32)
        return (x, ctx_2048, itok_Sx4_0_63)
    x, ctx_2048, itok_Sx4_0_63 = _rec_inputs()

    def _L0_attn_setup():
        import jax, jax.numpy as jnp
        import numpy as np
        H = 16
        DK = 96
        DV = 192
        HID = 512
        K = 4
        KEY_DIM = H * DK
        VAL_DIM = H * DV
        EPS = 1e-06

        def _causal_conv_silu(x, w):
            B, T, C = x.shape
            xt = x.transpose(0, 2, 1)
            out = jax.lax.conv_general_dilated(xt, w[:, None, :], window_strides=(1,), padding=[(K - 1, 0)], feature_group_count=C, dimension_numbers=('NCH', 'OIH', 'NCH'))
            return jax.nn.silu(out).transpose(0, 2, 1)

        def _l2norm(x):
            return x * jax.lax.rsqrt(jnp.sum(x * x, axis=-1, keepdims=True) + EPS)
        key = jax.random.key(seed)
        ks = jax.random.split(key, 16)
        std = 0.02
        return {'hidden_states': jax.random.normal(ks[0], (1, 256, HID), jnp.float32), 'Wq': jax.random.normal(ks[1], (HID, KEY_DIM), jnp.float32) * std, 'Wk': jax.random.normal(ks[2], (HID, KEY_DIM), jnp.float32) * std, 'Wv': jax.random.normal(ks[3], (HID, VAL_DIM), jnp.float32) * std, 'conv_q': jax.random.normal(ks[4], (KEY_DIM, K), jnp.float32) * 0.5, 'conv_k': jax.random.normal(ks[5], (KEY_DIM, K), jnp.float32) * 0.5, 'conv_v': jax.random.normal(ks[6], (VAL_DIM, K), jnp.float32) * 0.5, 'Wb': jax.random.normal(ks[7], (HID, H), jnp.float32) * std, 'Wa': jax.random.normal(ks[8], (HID, H), jnp.float32) * std, 'A_log': jnp.log(jnp.linspace(1.0, 8.0, H, dtype=jnp.float32)), 'dt_bias': jax.random.normal(ks[9], (H,), jnp.float32) * 0.5, 'Wg': jax.random.normal(ks[10], (HID, VAL_DIM), jnp.float32) * std, 'norm_weight': jnp.ones((DV,), jnp.float32), 'Wo': jax.random.normal(ks[11], (VAL_DIM, HID), jnp.float32) * std}
    _L0_attn_all = _L0_attn_setup()
    _L0_attn_in = {k: v for k, v in _L0_attn_all.items() if k in ('Wq', 'Wk', 'Wv', 'conv_q', 'conv_k', 'conv_v', 'Wb', 'Wa', 'A_log', 'dt_bias', 'Wg', 'norm_weight', 'Wo')}
    del _L0_attn_all

    def _L0_xattn_setup():
        import math
        import jax, jax.numpy as jnp
        import numpy as np
        B, S, D, N, K, TOPK = (4, 1024, 512, 64, 4, 2)
        key = jax.random.key(seed)
        k0, k1, k2, k3, k4 = jax.random.split(key, 5)
        token_states = jax.random.normal(k0, (B, S, D), dtype=jnp.float32)
        set_states = jax.random.normal(k1, (B, N, D), dtype=jnp.float32)
        desc_router = jax.random.normal(k2, (N, D), dtype=jnp.float32)
        token_to_sets = jax.random.randint(k3, (S, K), 0, N)
        bound = 1.0 / math.sqrt(D)
        W_q = jax.random.uniform(k4, (D, D), jnp.float32, -bound, bound)
        b_q = jnp.zeros((D,), jnp.float32)
        return {'token_states': token_states, 'set_states': set_states, 'desc_router': desc_router, 'W_q': W_q, 'b_q': b_q, 'token_to_sets': token_to_sets}
    _L0_xattn_all = _L0_xattn_setup()
    _L0_xattn_in = {k: v for k, v in _L0_xattn_all.items() if k in ('desc_router', 'W_q', 'b_q')}
    del _L0_xattn_all

    def _L0_ffn_setup():
        import jax, jax.numpy as jnp
        import numpy as np
        D_MODEL = 512
        HIDDEN = 4 * D_MODEL
        B, S = (2, 1024)

        def bit_linear(x, w, b):
            gamma_x = jnp.clip(jnp.max(jnp.abs(x), axis=-1, keepdims=True), 1e-05, None)
            scale_x = 127.0 / gamma_x
            x_dq = jnp.clip(jnp.round(x * scale_x), -128.0, 127.0) / scale_x
            x_ste = x + jax.lax.stop_gradient(x_dq - x)
            gamma_w = jnp.clip(jnp.mean(jnp.abs(w)), 1e-05, None)
            w_dq = jnp.clip(jnp.round(w / gamma_w), -1.0, 1.0) * gamma_w
            w_ste = w + jax.lax.stop_gradient(w_dq - w)
            return jnp.einsum('bsd,hd->bsh', x_ste, w_ste) + b
        key = jax.random.key(seed)
        ks = jax.random.split(key, 7)
        std = 0.02
        return {'x': jax.random.normal(ks[0], (B, S, D_MODEL), dtype=jnp.float32), 'gate_w': jax.random.normal(ks[1], (HIDDEN, D_MODEL), dtype=jnp.float32) * std, 'gate_b': jnp.zeros((HIDDEN,), dtype=jnp.float32), 'val_w': jax.random.normal(ks[2], (HIDDEN, D_MODEL), dtype=jnp.float32) * std, 'val_b': jnp.zeros((HIDDEN,), dtype=jnp.float32), 'out_w': jax.random.normal(ks[3], (D_MODEL, HIDDEN), dtype=jnp.float32) * std, 'out_b': jnp.zeros((D_MODEL,), dtype=jnp.float32)}
    _L0_ffn_all = _L0_ffn_setup()
    _L0_ffn_in = {k: v for k, v in _L0_ffn_all.items() if k in ('gate_w', 'gate_b', 'val_w', 'val_b', 'out_w', 'out_b')}
    del _L0_ffn_all
    return {'x': x, 'ctx_2048': ctx_2048, 'itok_Sx4_0_63': itok_Sx4_0_63, 'L0_attn_Wq': _L0_attn_in['Wq'], 'L0_attn_Wk': _L0_attn_in['Wk'], 'L0_attn_Wv': _L0_attn_in['Wv'], 'L0_attn_conv_q': _L0_attn_in['conv_q'], 'L0_attn_conv_k': _L0_attn_in['conv_k'], 'L0_attn_conv_v': _L0_attn_in['conv_v'], 'L0_attn_Wb': _L0_attn_in['Wb'], 'L0_attn_Wa': _L0_attn_in['Wa'], 'L0_attn_A_log': _L0_attn_in['A_log'], 'L0_attn_dt_bias': _L0_attn_in['dt_bias'], 'L0_attn_Wg': _L0_attn_in['Wg'], 'L0_attn_norm_weight': _L0_attn_in['norm_weight'], 'L0_attn_Wo': _L0_attn_in['Wo'], 'L0_xattn_desc_router': _L0_xattn_in['desc_router'], 'L0_xattn_W_q': _L0_xattn_in['W_q'], 'L0_xattn_b_q': _L0_xattn_in['b_q'], 'L0_ffn_gate_w': _L0_ffn_in['gate_w'], 'L0_ffn_gate_b': _L0_ffn_in['gate_b'], 'L0_ffn_val_w': _L0_ffn_in['val_w'], 'L0_ffn_val_b': _L0_ffn_in['val_b'], 'L0_ffn_out_w': _L0_ffn_in['out_w'], 'L0_ffn_out_b': _L0_ffn_in['out_b']}

def reference(x, ctx_2048, itok_Sx4_0_63, L0_attn_Wq, L0_attn_Wk, L0_attn_Wv, L0_attn_conv_q, L0_attn_conv_k, L0_attn_conv_v, L0_attn_Wb, L0_attn_Wa, L0_attn_A_log, L0_attn_dt_bias, L0_attn_Wg, L0_attn_norm_weight, L0_attn_Wo, L0_xattn_desc_router, L0_xattn_W_q, L0_xattn_b_q, L0_ffn_gate_w, L0_ffn_gate_b, L0_ffn_val_w, L0_ffn_val_b, L0_ffn_out_w, L0_ffn_out_b):
    import jax
    import jax.numpy as jnp

    def _L0_attn_ref(hidden_states, Wq, Wk, Wv, conv_q, conv_k, conv_v, Wb, Wa, A_log, dt_bias, Wg, norm_weight, Wo):
        import jax, jax.numpy as jnp
        import numpy as np
        H = 16
        DK = 96
        DV = 192
        HID = 512
        K = 4
        KEY_DIM = H * DK
        VAL_DIM = H * DV
        EPS = 1e-06

        def _causal_conv_silu(x, w):
            B, T, C = x.shape
            xt = x.transpose(0, 2, 1)
            out = jax.lax.conv_general_dilated(xt, w[:, None, :], window_strides=(1,), padding=[(K - 1, 0)], feature_group_count=C, dimension_numbers=('NCH', 'OIH', 'NCH'))
            return jax.nn.silu(out).transpose(0, 2, 1)

        def _l2norm(x):
            return x * jax.lax.rsqrt(jnp.sum(x * x, axis=-1, keepdims=True) + EPS)
        B, T, _ = hidden_states.shape
        q = _causal_conv_silu(hidden_states @ Wq, conv_q).reshape(B, T, H, DK)
        k = _causal_conv_silu(hidden_states @ Wk, conv_k).reshape(B, T, H, DK)
        v = _causal_conv_silu(hidden_states @ Wv, conv_v).reshape(B, T, H, DV)
        q = _l2norm(q) * DK ** (-0.5)
        k = _l2norm(k)
        beta = jax.nn.sigmoid(hidden_states @ Wb) * 2.0
        g = -jnp.exp(A_log) * jax.nn.softplus(hidden_states @ Wa + dt_bias)

        def step(S, inp):
            q_t, k_t, v_t, g_t, b_t = inp
            S = S * jnp.exp(g_t)[..., None, None]
            kv = jnp.einsum('bhk,bhkv->bhv', k_t, S)
            delta = (v_t - kv) * b_t[..., None]
            S = S + jnp.einsum('bhk,bhv->bhkv', k_t, delta)
            o = jnp.einsum('bhk,bhkv->bhv', q_t, S)
            return (S, o)
        S0 = jnp.zeros((B, H, DK, DV), hidden_states.dtype)
        xs = (q.transpose(1, 0, 2, 3), k.transpose(1, 0, 2, 3), v.transpose(1, 0, 2, 3), g.transpose(1, 0, 2), beta.transpose(1, 0, 2))
        _, o = jax.lax.scan(step, S0, xs)
        o = o.transpose(1, 0, 2, 3)
        gate = (hidden_states @ Wg).reshape(B, T, H, DV)
        var = jnp.mean(o * o, axis=-1, keepdims=True)
        o = o * jax.lax.rsqrt(var + EPS) * norm_weight * jax.nn.silu(gate)
        return o.reshape(B, T, VAL_DIM) @ Wo

    def _L0_xattn_ref(token_states, set_states, desc_router, W_q, b_q, token_to_sets):
        import math
        import jax, jax.numpy as jnp
        import numpy as np
        B, S, D, N, K, TOPK = (4, 1024, 512, 64, 4, 2)
        batch, seq_len, d = token_states.shape
        num_sets = set_states.shape[1]
        scale = 1.0 / math.sqrt(d)
        q = jnp.einsum('bsd,ed->bse', token_states, W_q) + b_q
        scores = jnp.einsum('bse,ne->bsn', q, desc_router) * scale
        valid = token_to_sets >= 0
        mask = ((token_to_sets[:, :, None] == jnp.arange(num_sets)[None, None, :]) & valid[:, :, None]).any(axis=1)
        neg_inf = jnp.array(-jnp.inf, scores.dtype)
        scores = jnp.where(mask[None, :, :], scores, neg_inf)
        topk_vals, topk_idx = jax.lax.top_k(scores, TOPK)
        b_i = jnp.arange(batch)[:, None, None]
        s_i = jnp.arange(seq_len)[None, :, None]
        scores = jnp.full_like(scores, neg_inf).at[b_i, s_i, topk_idx].set(topk_vals)
        weights = jax.nn.softmax(scores, axis=-1)
        return jnp.einsum('bsn,bnd->bsd', weights, set_states)

    def _L0_ffn_ref(x, gate_w, gate_b, val_w, val_b, out_w, out_b):
        import jax, jax.numpy as jnp
        import numpy as np
        D_MODEL = 512
        HIDDEN = 4 * D_MODEL
        B, S = (2, 1024)

        def bit_linear(x, w, b):
            gamma_x = jnp.clip(jnp.max(jnp.abs(x), axis=-1, keepdims=True), 1e-05, None)
            scale_x = 127.0 / gamma_x
            x_dq = jnp.clip(jnp.round(x * scale_x), -128.0, 127.0) / scale_x
            x_ste = x + jax.lax.stop_gradient(x_dq - x)
            gamma_w = jnp.clip(jnp.mean(jnp.abs(w)), 1e-05, None)
            w_dq = jnp.clip(jnp.round(w / gamma_w), -1.0, 1.0) * gamma_w
            w_ste = w + jax.lax.stop_gradient(w_dq - w)
            return jnp.einsum('bsd,hd->bsh', x_ste, w_ste) + b
        gate = jax.nn.silu(bit_linear(x, gate_w, gate_b))
        val = bit_linear(x, val_w, val_b)
        return bit_linear(gate * val, out_w, out_b)
    x = x + _L0_attn_ref(_layernorm(x, axis=-1), L0_attn_Wq, L0_attn_Wk, L0_attn_Wv, L0_attn_conv_q, L0_attn_conv_k, L0_attn_conv_v, L0_attn_Wb, L0_attn_Wa, L0_attn_A_log, L0_attn_dt_bias, L0_attn_Wg, L0_attn_norm_weight, L0_attn_Wo)
    x = x + _L0_xattn_ref(_layernorm(x, axis=-1), ctx_2048, L0_xattn_desc_router, L0_xattn_W_q, L0_xattn_b_q, itok_Sx4_0_63)
    x = x + _L0_ffn_ref(_layernorm(x, axis=-1), L0_ffn_gate_w, L0_ffn_gate_b, L0_ffn_val_w, L0_ffn_val_b, L0_ffn_out_w, L0_ffn_out_b)
    return x

_drawn_inputs = setup_inputs


def setup_inputs(seed=0):
    import zlib

    import numpy as np

    out = dict(_drawn_inputs(seed))
    spreads = {'L0_attn_norm_weight': (1.0, 0.2),
     'L0_xattn_b_q': (0.0, 0.1),
     'L0_ffn_gate_b': (0.0, 0.8),
     'L0_ffn_val_b': (0.0, 0.8),
     'L0_ffn_out_b': (0.0, 0.1)}
    factors = {}
    for name, (base, spread) in spreads.items():
        noise = np.random.default_rng([zlib.crc32(name.encode()), seed]).standard_normal(out[name].shape)
        drawn = base * np.exp(spread * noise) if base else spread * noise
        out[name] = jnp.asarray(drawn.astype(out[name].dtype))
    for name, factor in factors.items():
        out[name] = (out[name] * factor).astype(out[name].dtype)
    return out
```

```python
from contextlib import ExitStack

import numpy as np

import concourse.bass as bass
from concourse import mybir

P = 128
F32 = mybir.dt.float32
F16 = mybir.dt.float16
BF16 = mybir.dt.bfloat16
I32 = mybir.dt.int32
U32 = mybir.dt.uint32
ALU = mybir.AluOpType
ACT = mybir.ActivationFunctionType
AXX = mybir.AxisListType.X
ds = bass.ds

B, T, D = 4, 512, 512
H, DK, DV = 16, 96, 192
KC = D // P
NT = B * T // P
CH = T // P
HB = P // 2
LV = 6
QKV = 2 * DK + DV
NS = H * CH
FF = 4 * D
NSET = 64
TOPK_IN = 4
SH, SW = 64.0, 1024.0
SHW = SH * SW
LN_EPS, EPS = 1e-5, 1e-6
ROUND = 12582912.0
G_, BETA, NBETA, EG, NBEG = range(5)

C_U, C_GT, C_ID = 0, P, 2 * P
C_M = 3 * P
C_I64 = C_M + (LV + 1) * HB
C_IOTA = C_I64 + HB
C_ALL = C_IOTA + NSET


def shape_constants():
    c = np.zeros((P, C_ALL), np.float32)
    r = np.arange(P)[:, None]
    t = np.arange(P)[None, :]
    c[:, C_U:C_U + P] = r <= t
    c[:, C_GT:C_GT + P] = r > t
    c[:, C_ID:C_ID + P] = r == t
    h = np.arange(HB)[None, :]
    for lv in range(LV):
        s = 1 << lv
        c[:, C_M + lv * HB:C_M + (lv + 1) * HB] = ((r % HB) // s % 2 == 1) & (h // s == (r % HB) // s - 1)
    c[:, C_M + LV * HB:C_M + (LV + 1) * HB] = r >= HB
    c[:, C_I64:C_I64 + HB] = (r % HB) == h
    c[:, C_IOTA:C_IOTA + NSET] = np.arange(NSET)[None, :]
    return c


def over(ap, axis, n):
    a = ap.unsqueeze(axis)
    shape = list(a.shape)
    shape[axis] = n
    return a.broadcast_to(shape)


def tile_pairs(eng, body):
    body(0)
    with eng.Fori(1, NT // 2) as i:
        body(i)


def stage_norm_and_scalars(nc, io, keep):
    x_sb, hhi, hlo, sc, dec, cst, bank = (keep[k] for k in ("x", "hhi", "hlo", "sc", "dec", "cst", "bank"))
    with ExitStack() as ctx:
        def sb(name, shape, dt=F32):
            return ctx.enter_context(nc.sbuf_tensor("n_" + name, shape, dt))

        def sem(name):
            return ctx.enter_context(nc.semaphore("n_" + name))

        stats = sb("stats", [P, 6])
        mv = sb("mv", [P, NT, 2])
        var = sb("var", [P, NT])
        half = sb("half", [P, NT])
        rstd = sb("rstd", [P, NT])
        hn = [sb(f"hn{p}", [P, D]) for p in range(2)]
        wab = sb("wab", [P, KC, 2 * H])
        wabh = sb("wabh", [P, KC, 2 * H], F16)
        wabl = sb("wabl", [P, KC, 2 * H], F16)
        dtb = sb("dtb", [P, H])
        alog = sb("alog", [P, H])
        z = sb("z", [P, NT, H])
        az = sb("az", [P, NT, H])
        ez = sb("ez", [P, NT, H])
        lz = sb("lz", [P, NT, H])
        rz = sb("rz", [P, NT, H])
        eb = sb("eb", [P, NT, H])
        bt = sb("bt", [P, NT, H])
        ones = sb("ones", [P, P])
        x_in = [sem(f"x_in{b}") for b in range(B)]
        par_in = sem("par_in")
        cst_in = sem("cst_in")
        stat = sem("stat")
        rstd_ready = sem("rstd_ready")
        hn_ready = [sem(f"hn_ready{p}") for p in range(2)]
        hT_ready = [sem(f"hT_ready{p}") for p in range(2)]
        hi_ready = [sem(f"hi_ready{p}") for p in range(2)]
        lo_ready = [sem(f"lo_ready{p}") for p in range(2)]
        wab_ready = sem("wab_ready")
        ab_ready = sem("ab_ready")
        v_small = sem("v_small")
        a_small = sem("a_small")
        g_small = sem("g_small")
        sum_ready = sem("sum_ready")
        block = ctx.enter_context(nc.Block())

        @block.sync
        def _(sp):
            for b in range(B):
                sp.dma_start(x_sb[:, b * CH:(b + 1) * CH, :], io["x"][b].rearrange("(c p) d -> p c d", p=P)).then_inc(x_in[b], 16)
                if b == 0:
                    sp.dma_start(cst[:, :], io["cst"]).then_inc(cst_in, 16)
            sp.dma_start(wab[:, :, 0:H], io["L0_attn_Wa"].rearrange("(k p) h -> p k h", p=P)).then_inc(par_in, 16)
            sp.dma_start(wab[:, :, H:], io["L0_attn_Wb"].rearrange("(k p) h -> p k h", p=P)).then_inc(par_in, 16)
            sp.dma_start(dtb[:, :], io["L0_attn_dt_bias"].partition_broadcast(P)).then_inc(par_in, 16)
            sp.dma_start(alog[:, :], io["L0_attn_A_log"].partition_broadcast(P)).then_inc(par_in, 16)

        @block.gpsimd
        def _(pool):
            nc.gpsimd.memset(ones[:, :], 1.0).then_inc(g_small, 1)
            nc.gpsimd.memset(half[:, :], -0.5).then_inc(g_small, 1)
            pool.wait_ge(stat, 2 * NT)
            nc.gpsimd.tensor_scalar(var[:, :], mv[:, :, 1], LN_EPS, None, ALU.add).then_inc(g_small, 1)
            pool.wait_ge(g_small, 3)
            nc.gpsimd.tensor_tensor(rstd[:, :], var[:, :], half[:, :], ALU.pow).then_inc(rstd_ready, 1)
            pool.wait_ge(par_in, 64)
            nc.gpsimd.tensor_scalar(wab[:, :, :], wab[:, :, :], SW, None, ALU.mult).then_inc(g_small, 1)
            pool.wait_ge(g_small, 4)
            nc.gpsimd.tensor_copy(wabh[:, :, :], wab[:, :, :]).then_inc(g_small, 1)
            pool.wait_ge(g_small, 5)
            nc.gpsimd.tensor_tensor(wabl[:, :, :], wab[:, :, :], wabh[:, :, :], ALU.subtract).then_inc(wab_ready, 1)

        @block.vector
        def _(v):
            for t in range(NT):
                if t % CH == 0:
                    v.wait_ge(x_in[t // CH], 16)
                if t:
                    v.wait_ge(stat, 2 * t)
                nc.vector.bn_stats(stats[:, :], x_sb[:, t, :]).then_inc(stat, 1)
                v.wait_ge(stat, 2 * t + 1)
                nc.vector.bn_aggr(mv[:, t, :], stats[:, :]).then_inc(stat, 1)
            v.wait_ge(rstd_ready, 1)
            v.wait_ge(stat, 2 * NT)
            def pair(i):
                for p in range(2):
                    v.wait_ge(hT_ready[p], i)
                    nc.vector.tensor_scalar(hn[p][:, :], x_sb[:, ds(i * 2 + p, 1), :].squeeze(1), mv[:, ds(i * 2 + p, 1), 0],
                                            rstd[:, ds(i * 2 + p, 1)], ALU.subtract, ALU.mult).then_inc(hn_ready[p], 1)
                for p in range(2):
                    v.wait_ge(hi_ready[p], i + 1)
                    hs = ds((i * 2 + p) * P, P)
                    nc.vector.scalar_tensor_tensor(out=hlo[:, :, hs], in0=bank[p][:, :].rearrange("p (k t) -> p k t", k=KC),
                                                   scalar=SH, in1=hhi[:, :, hs], op0=ALU.mult, op1=ALU.subtract).then_inc(lo_ready[p], 1)

            tile_pairs(v, pair)
            v.wait_ge(ab_ready, 1)
            v.wait_ge(par_in, 64)
            ab = bank[2][:, :].rearrange("p (t h) -> p t h", t=NT)
            nc.vector.scalar_tensor_tensor(out=z[:, :, :], in0=ab[:, :, 0:H], scalar=1.0 / SHW, in1=over(dtb[:, :], 1, NT),
                                           op0=ALU.mult, op1=ALU.add).then_inc(v_small, 1)
            v.wait_ge(v_small, 1)
            nc.vector.tensor_scalar(az[:, :, :], z[:, :, :], -1.0, None, ALU.mult).then_inc(v_small, 1)
            v.wait_ge(v_small, 2)
            nc.vector.tensor_tensor(az[:, :, :], az[:, :, :], z[:, :, :], ALU.min).then_inc(v_small, 1)
            nc.vector.tensor_scalar(rz[:, :, :], z[:, :, :], 0.0, None, ALU.max).then_inc(v_small, 1)
            v.wait_ge(a_small, 4)
            v.wait_ge(v_small, 4)
            nc.vector.tensor_tensor(rz[:, :, :], rz[:, :, :], lz[:, :, :], ALU.add).then_inc(v_small, 1)
            v.wait_ge(v_small, 5)
            g_view = sc[:, G_, :, :].rearrange("p (h c) b -> p b c h", c=CH)
            for b in range(B):
                nc.vector.scalar_tensor_tensor(out=g_view[:, b], in0=rz[:, b * CH:(b + 1) * CH, :], scalar=-1.0,
                                               in1=over(alog[:, :], 1, CH), op0=ALU.mult, op1=ALU.mult).then_inc(v_small, 1)
            nc.vector.tensor_scalar(eb[:, :, :], eb[:, :, :], 1.0, None, ALU.add).then_inc(v_small, 1)
            v.wait_ge(v_small, 10)
            nc.vector.reciprocal(bt[:, :, :], eb[:, :, :]).then_inc(v_small, 1)
            v.wait_ge(v_small, 11)
            for kind, factor in ((BETA, 2.0), (NBETA, -2.0)):
                view = sc[:, kind, :, :].rearrange("p (h c) b -> p b c h", c=CH)
                for b in range(B):
                    nc.vector.tensor_scalar(view[:, b], bt[:, b * CH:(b + 1) * CH, :], factor, None, ALU.mult).then_inc(v_small, 1)
            v.wait_ge(a_small, 5)
            v.wait_ge(v_small, 19)
            nc.vector.tensor_tensor(sc[:, NBEG, :, :], sc[:, NBETA, :, :], sc[:, EG, :, :], ALU.mult).then_inc(v_small, 1)

        @block.scalar
        def _(a):
            def pair(i):
                for p in range(2):
                    a.wait_ge(hT_ready[p], i + 1)
                    nc.scalar.activation(hhi[:, :, ds((i * 2 + p) * P, P)], bank[p][:, :].rearrange("p (k t) -> p k t", k=KC),
                                         ACT.Copy, scale=SH).then_inc(hi_ready[p], 1)

            tile_pairs(a, pair)
            a.wait_ge(par_in, 64)
            a.wait_ge(v_small, 4)
            nc.scalar.activation(ez[:, :, :], az[:, :, :], ACT.Exp).then_inc(a_small, 1)
            a.wait_ge(a_small, 1)
            nc.scalar.activation(lz[:, :, :], ez[:, :, :], ACT.Ln, bias=1.0).then_inc(a_small, 1)
            nc.scalar.activation(alog[:, :], alog[:, :], ACT.Exp).then_inc(a_small, 1)
            nc.scalar.activation(eb[:, :, :], bank[2][:, :].rearrange("p (t h) -> p t h", t=NT)[:, :, H:], ACT.Exp,
                                 scale=-1.0 / SHW).then_inc(a_small, 1)
            a.wait_ge(sum_ready, 1)
            nc.scalar.activation(sc[:, EG, :, :].rearrange("p n b -> p (n b)"), bank[3][:, 0:NS * B], ACT.Exp).then_inc(a_small, 1)
            nc.scalar.activation(dec[:, :, :].rearrange("p n b -> p (n b)"), bank[3][:, NS * B:], ACT.Exp).then_inc(a_small, 1)

        @block.tensor
        def _(pe):
            pe.wait_ge(cst_in, 16)
            def pair(i):
                for p in range(2):
                    pe.wait_ge(hn_ready[p], i + 1)
                    pe.wait_ge(lo_ready[p], i)
                    for k in range(KC):
                        last = nc.tensor.transpose(bank[p][:, k * P:(k + 1) * P], hn[p][:, k * P:(k + 1) * P], cst[:, C_ID:C_ID + P])
                    last.then_inc(hT_ready[p], 1)

            tile_pairs(pe, pair)
            for p in range(2):
                pe.wait_ge(lo_ready[p], NT // 2)
            pe.wait_ge(wab_ready, 1)
            for t in range(NT):
                terms = [(x, w, k) for x, w in ((hhi, wabh), (hhi, wabl), (hlo, wabh)) for k in range(KC)]
                for n, (x, w, k) in enumerate(terms):
                    last = nc.tensor.matmul(bank[2][:, t * 2 * H:(t + 1) * 2 * H], x[:, k, t * P:(t + 1) * P], w[:, k, :],
                                            start=(n == 0), stop=(n == len(terms) - 1))
            last.then_inc(ab_ready, 1)
            pe.wait_ge(v_small, 9)
            pe.wait_ge(g_small, 1)
            g_all = sc[:, G_, :, :].rearrange("p n b -> p (n b)")
            nc.tensor.matmul(bank[3][:, 0:NS * B], cst[:, C_U:C_U + P], g_all, start=True, stop=True)
            nc.tensor.matmul(bank[3][:, NS * B:], ones[:, :], g_all, start=True, stop=True).then_inc(sum_ready, 1)


class Step:

    def __init__(self, n, k, u, project, recur):
        self.n, self.m, self.k, self.c = n, n + 1, k, u % CH
        self.ka = k + 1 if self.c == CH - 1 else k
        self.cm = (u + 1) % CH
        self.p, self.pm = u % 2, (u + 1) % 2
        self.wq = ((u + 1) // CH) % 2
        self.p_head = (u // CH) % 2
        self.project, self.recur = project, recur


def all_steps(eng, body):
    body(Step(-1, -1, -1, True, False))
    for u in range(2 * CH):
        body(Step(u, u // CH, u, True, True))
    with eng.Fori(1, H // 2 - 1) as j:
        for u in range(2 * CH):
            body(Step(j * (2 * CH) + u, j * 2 + u // CH, u, True, True))
    for u in range(2 * CH):
        n = NS - 2 * CH + u
        body(Step(n, n // CH, u, n + 1 < NS, True))


def stage_delta_rule(nc, io, keep):
    x_sb, hhi, hlo, sc, dec, cst, bank = (keep[k] for k in ("x", "hhi", "hlo", "sc", "dec", "cst", "bank"))
    with ExitStack() as ctx:
        def sb(name, shape, dt=F32):
            return ctx.enter_context(nc.sbuf_tensor("d_" + name, shape, dt))

        def sem(name):
            return ctx.enter_context(nc.semaphore("d_" + name))

        st = sb("st", [P, KC * DV + 2 * D])
        st_a = st[:, 0:KC * QKV].rearrange("p (k n) -> p k n", k=KC)
        st_g = st[:, 0:KC * DV].rearrange("p (k n) -> p k n", k=KC)
        st_o = st[0:DK, KC * DV:].rearrange("p (i n) -> p i n", i=2)
        wa = [[sb(f"wa{q}{s}", [P, KC, QKV], F16) for s in "hl"] for q in range(2)]
        wg = [sb(f"wg{s}", [P, KC, DV], F16) for s in "hl"]
        wo = sb("wo", [DK, 2, D])
        nw = sb("nw", [DK, 2])
        cw = sb("cw", [P, H, 3, 4])
        y = [sb(f"y{q}", [P, B, P]) for q in range(2)]
        th = sb("th", [P, B, P])
        qT = [sb(f"qT{q}", [P, B, P]) for q in range(2)]
        yv = sb("yv", [P, 2, B, P])
        tail = [sb(f"tail{q}", [P, 3, B, 3]) for q in range(2)]
        tok = sb("tok", [P, B, QKV])
        sq = sb("sq", [P, B, 2, DK])
        ss = sb("ss", [P, B, 2])
        sse = sb("sse", [P, B, 2])
        kap = sb("kap", [P, B, 2])
        mhalf = sb("mhalf", [P, B, 2])
        epsq = [sb(f"epsq{q}", [P, B]) for q in range(2)]
        V = [sb(f"V{q}", [P, B, DV]) for q in range(2)]
        K = [sb(f"K{q}", [P, B, DK]) for q in range(2)]
        kT = [sb(f"kT{q}", [DK, B, P]) for q in range(2)]
        Gm = sb("Gm", [P, B, P])
        E = sb("E", [P, B, P])
        Em = sb("Em", [P, B, P])
        LT = sb("LT", [P, B, P])
        PT = sb("PT", [P, B, P])
        nbM = sb("nbM", [P, LV + 1, B, HB])
        Y = sb("Y", [P, B * HB])
        X = sb("X", [P, 2 * B * HB])
        XT = sb("XT", [P, B, P])
        i8 = sb("i8", [P, 2 * B, HB], BF16)
        idb = sb("idb", [P, P], BF16)
        S = sb("S", [DK, B, DV])
        W = sb("W", [P, B, DV])
        Q = sb("Q", [P, B, DV])
        Dl = sb("Dl", [P, B, DV])
        K2 = sb("K2", [P, B, DK])
        thg = sb("thg", [P, 2 * DV])
        gate = sb("gate", [P, B, DV])
        O = W
        on = Q
        junk = sb("junk", [P, B, DV])
        sso = sb("sso", [P, B])
        ms = sb("ms", [P, B])
        rn = sb("rn", [P, B])
        onT = sb("onT", [DK, 2, B, P])

        names = """par_in st_a_in st_g_in st_o_in wa_scaled wg_scaled
            const_ready cw_ready wa_ready wg_ready wo_ready
            proj_done tap0_done conv_done tanh_done silu_done tok_done tok_read sq_done ss_done kappa_done V_ready K_ready
            kT_done kT_ready
            Gm_ready nbM_ready dif_done E_ready Em_ready gram_done qk_done LT_ready PT_ready
            ks_done qs_done W_ready qs_read yps_done Y_ready xps_done X_ready x21_done XT_ready
            gate_done gtanh_done gate_ready d_done D_ready pd_done O_ready K2_ready su_done S_ready
            ssq_done r_ready on_ready onT_done onT_ready wo_done x_added""".split()
        s = {name: sem(name) for name in names}
        block = ctx.enter_context(nc.Block())
        ident = cst[:, C_ID:C_ID + P]
        U = cst[:, C_U:C_U + P]

        held = {str(e.engine): sem(name + "_held") for name, e in (("pe", nc.tensor), ("act", nc.scalar), ("pool", nc.gpsimd), ("sp", nc.sync))}

        def hold(eng, sem, value):
            eng.wait_ge(sem, value)
            if not isinstance(value, int):
                eng.sem_inc(held[str(eng.engine)], 1)

        @block.sync
        def _(sp):
            def load_a(h):
                if not isinstance(h, int) or h > 0:
                    hold(sp, s["wa_ready"], h)
                if not isinstance(h, int):
                    hold(sp, s["wg_ready"], h - 1)
                    hold(sp, s["wo_ready"], h - 1)
                for name, at, w in (("Wq", 0, DK), ("Wv", DK, DV), ("Wk", DK + DV, DK)):
                    src = io["L0_attn_" + name].rearrange("(k p) n -> p k n", p=P)
                    sp.dma_start(st_a[:, :, at:at + w], src[:, :, ds(h * w, w)]).then_inc(s["st_a_in"], 16)

            for i in range(2):
                sp.dma_start(nw[:, i:i + 1], io["L0_attn_norm_weight"].rearrange("(i p) -> p i", i=2)[:, i:i + 1]).then_inc(s["par_in"], 16)
            cq, ck, cv = (io["L0_attn_conv_" + n].rearrange("(h c) k -> c h k", h=H) for n in "qkv")
            v0, v1 = P - DK, 2 * P - DK
            sp.dma_start(cw[0:DK, :, 0, :], cq).then_inc(s["par_in"], 16)
            sp.dma_start(cw[DK:P, :, 0, :], cv[0:v0]).then_inc(s["par_in"], 16)
            sp.dma_start(cw[:, :, 1, :], cv[v0:v1]).then_inc(s["par_in"], 16)
            sp.dma_start(cw[0:P - DK, :, 2, :], cv[v1:DV]).then_inc(s["par_in"], 16)
            sp.dma_start(cw[P - DK:P, :, 2, :], ck).then_inc(s["par_in"], 16)
            load_a(0)
            load_a(1)

            def load_go(k):
                if isinstance(k, int):
                    hold(sp, s["wg_ready"], k)
                    hold(sp, s["wo_ready"], k)
                else:
                    hold(sp, s["wa_ready"], k + 2)
                sp.dma_start(st_g, io["L0_attn_Wg"].rearrange("(k p) n -> p k n", p=P)[:, :, ds(k * DV, DV)]).then_inc(s["st_g_in"], 16)
                sp.dma_start(st_o, io["L0_attn_Wo"].rearrange("(k p) n -> p k n", p=DK)[:, ds(k * 2, 2), :]).then_inc(s["st_o_in"], 16)

            with sp.Fori(0, H - 2) as k:
                load_go(k)
                load_a(k + 2)
            sp.wait_ge(s["wa_ready"], H)
            for k in range(H - 2, H):
                load_go(k)

        @block.gpsimd
        def _(pool):
            def prepare():
                nc.gpsimd.memset(mhalf[:, :, :], -0.5).then_inc(s["const_ready"], 1)
                nc.gpsimd.memset(XT[:, :, :], 0.0).then_inc(s["const_ready"], 1)
                nc.gpsimd.tensor_copy(i8[:, :, :], over(cst[:, C_I64:C_I64 + HB], 1, 2 * B)).then_inc(s["const_ready"], 1)
                nc.gpsimd.tensor_copy(idb[:, :], ident).then_inc(s["const_ready"], 1)
                hold(pool, s["par_in"], 16 * 7)
                nc.gpsimd.tensor_scalar(cw[:, :, :, :], cw[:, :, :, :], 0.5 / SHW, None, ALU.mult).then_inc(s["cw_ready"], 1)
                nc.gpsimd.tensor_scalar(nw[:, :], nw[:, :], 0.5 / SHW, None, ALU.mult).then_inc(s["cw_ready"], 1)

            def split_a(h, q):
                hold(pool, s["st_a_in"], (h + 1) * 48)
                if not isinstance(h, int) or h >= 2:
                    hold(pool, s["proj_done"], (h - 1) * 3 * CH)
                scaled = s["wa_scaled"]
                nc.gpsimd.tensor_scalar(st_a[:, :, :], st_a[:, :, :], SW, None, ALU.mult).then_inc(scaled, 1)
                hold(pool, scaled, h * 2 + 1)
                nc.gpsimd.tensor_copy(wa[q][0][:, :, :], st_a[:, :, :]).then_inc(scaled, 1)
                hold(pool, scaled, h * 2 + 2)
                nc.gpsimd.tensor_tensor(wa[q][1][:, :, :], st_a[:, :, :], wa[q][0][:, :, :], ALU.subtract).then_inc(s["wa_ready"], 1)

            def split_g(k):
                hold(pool, s["st_g_in"], k * 16 + 16)
                hold(pool, s["gate_done"], 2 * CH * k)
                nc.gpsimd.tensor_scalar(st_g[:, :, :], st_g[:, :, :], SW, None, ALU.mult).then_inc(s["wg_scaled"], 1)
                hold(pool, s["wg_scaled"], k * 2 + 1)
                nc.gpsimd.tensor_copy(wg[0][:, :, :], st_g[:, :, :]).then_inc(s["wg_scaled"], 1)
                hold(pool, s["wg_scaled"], k * 2 + 2)
                nc.gpsimd.tensor_tensor(wg[1][:, :, :], st_g[:, :, :], wg[0][:, :, :], ALU.subtract).then_inc(s["wg_ready"], 1)

            def scale_o(k):
                hold(pool, s["st_o_in"], k * 16 + 16)
                hold(pool, s["wo_done"], B * CH * k)
                for i in range(2):
                    last = nc.gpsimd.tensor_scalar(wo[:, i, :], st_o[:, i, :], nw[:, i:i + 1], None, ALU.mult)
                last.then_inc(s["wo_ready"], 1)

            def step(st):
                n, m, c = st.n, st.m, st.c
                if st.recur:
                    hold(pool, s["dif_done"], n)
                    nc.gpsimd.tensor_tensor(Gm[:, :, :], over(U, 1, B),
                                            over(sc[:, G_, ds(n, 1), :].squeeze(1), 2, P), ALU.mult).then_inc(s["Gm_ready"], 1)
                    hold(pool, s["XT_ready"], n)
                    for l in range(LV + 1):
                        last = nc.gpsimd.tensor_tensor(nbM[:, l, :, :], over(cst[:, C_M + l * HB:C_M + (l + 1) * HB], 1, B),
                                                       over(sc[:, NBETA, ds(n, 1), :].squeeze(1), 2, HB), ALU.mult)
                    last.then_inc(s["nbM_ready"], 1)
                    hold(pool, s["E_ready"], n + 1)
                    hold(pool, s["PT_ready"], n)
                    nc.gpsimd.tensor_tensor(Em[:, :, :], E[:, :, :], over(U, 1, B), ALU.mult).then_inc(s["Em_ready"], 1)
                    hold(pool, s["su_done"], 2 * n)
                    for i in range(B):
                        nc.gpsimd.tensor_scalar(K2[:, i, :], K[st.p][:, i, :], E[:, i, P - 1:P], None, ALU.mult).then_inc(s["K2_ready"], 1)
                    if c == 0:
                        split_g(st.k)
                        scale_o(st.k)
                if st.project:
                    if c == CH - 1 and not (isinstance(n, int) and st.k + 2 >= H):
                        split_a(st.k + 2, st.p_head)
                    hold(pool, s["tok_read"], B * m + B)
                    hold(pool, s["ss_done"], m)
                    for i, at in ((0, 0), (1, DK + DV)):
                        last = nc.gpsimd.tensor_tensor(sq[:, :, i, :], tok[:, :, at:at + DK], tok[:, :, at:at + DK], ALU.mult)
                    last.then_inc(s["sq_done"], 1)
                    if st.recur:
                        hold(pool, s["W_ready"], B * n)
                    nc.gpsimd.tensor_tensor(V[st.pm][:, :, :], tok[:, :, DK:DK + DV],
                                            over(sc[:, BETA, ds(m, 1), :].squeeze(1), 2, DV), ALU.mult).then_inc(s["V_ready"], 1)
                    hold(pool, s["ss_done"], m + 1)
                    nc.gpsimd.tensor_scalar(sse[:, :, :], ss[:, :, :], EPS, None, ALU.add).then_inc(s["kappa_done"], 1)
                    hold(pool, s["kappa_done"], 3 * m + 1)
                    nc.gpsimd.tensor_tensor(kap[:, :, :], sse[:, :, :], mhalf[:, :, :], ALU.pow).then_inc(s["kappa_done"], 1)
                    nc.gpsimd.tensor_scalar(epsq[st.pm][:, :], sse[:, :, 0], EPS * DK, None, ALU.mult).then_inc(s["kappa_done"], 1)
                    hold(pool, s["kappa_done"], 3 * m + 3)
                    nc.gpsimd.tensor_tensor(K[st.pm][:, :, :], tok[:, :, DK + DV:], over(kap[:, :, 1], 2, DK),
                                            ALU.mult).then_inc(s["K_ready"], 1)
                if st.recur:
                    hold(pool, s["ssq_done"], B * n + B)
                    nc.gpsimd.tensor_scalar(ms[:, :], sso[:, :], 1.0 / DV, None, ALU.mult).then_inc(s["r_ready"], 1)
                    hold(pool, s["r_ready"], 3 * n + 1)
                    nc.gpsimd.tensor_tensor(ms[:, :], ms[:, :], epsq[st.p][:, :], ALU.add).then_inc(s["r_ready"], 1)
                    hold(pool, s["r_ready"], 3 * n + 2)
                    nc.gpsimd.tensor_tensor(rn[:, :], ms[:, :], mhalf[:, 0:2, :].rearrange("p a b -> p (a b)"), ALU.pow).then_inc(s["r_ready"], 1)

            prepare()
            hold(pool, s["const_ready"], 4)
            hold(pool, s["cw_ready"], 2)
            split_a(0, 0)
            all_steps(pool, step)

        @block.tensor
        def _(pe):
            pe.wait_ge(s["const_ready"], 4)

            def projection(st, t, part):
                m = st.m
                acc = bank[(st.pm + t) % 2]
                if t == 0 and st.cm == 0 and part == 0:
                    pe.wait_ge(s["wa_ready"], st.ka + 1)
                if part == 0 and not (isinstance(m, int) and 3 * m + t < 2):
                    pe.wait_ge(s["conv_done"], 7 * (3 * m + t - 1))
                w, x = ((0, hhi), (1, hhi), (0, hlo))[part]
                for k in range(KC):
                    last = nc.tensor.matmul(acc[:, :], wa[st.wq][w][:, k, t * P:(t + 1) * P],
                                            x[:, k, :].rearrange("p (b t) -> p b t", b=B)[:, :, st.cm * P:(st.cm + 1) * P],
                                            start=(part == 0 and k == 0), stop=(part == 2 and k == KC - 1))
                if part == 2:
                    last.then_inc(s["proj_done"], 1)

            def to_tokens(st, i):
                m = st.m
                if i == 0:
                    pe.wait_ge(s["silu_done"], 3 * m + 3)
                    pe.wait_ge(s["kT_ready"], m)
                pe.wait_ge(s["tok_read"], B * m + i)
                for t in range(3):
                    src = qT[st.pm][:, i, :] if t == 0 else yv[:, t - 1, i, :]
                    last = nc.tensor.transpose(bank[2][:, t * P:(t + 1) * P], src, ident)
                last.then_inc(s["tok_done"], 1)

            def keys_back(st):
                m = st.m
                pe.wait_ge(s["K_ready"], m + 1)
                pe.wait_ge(s["tok_read"], B * m + B)
                for i in range(B):
                    last = nc.tensor.transpose(bank[2][0:DK, i * P:(i + 1) * P], K[st.pm][:, i, :], ident)
                last.then_inc(s["kT_done"], 1)

            def levels(st, fill):
                n = st.n
                yb, xb = bank[3], bank[4]
                half = (slice(0, HB), slice(HB, P))
                i64 = cst[:, C_I64:C_I64 + HB]
                for l in range(LV):
                    if l == 0:
                        hold(pe, s["LT_ready"], n + 1)
                        hold(pe, s["XT_ready"], n)
                    else:
                        hold(pe, s["X_ready"], 8 * n + l)
                    for i in range(B):
                        for hf in half:
                            rhs = i64[hf, :] if l == 0 else X[hf, i * HB:(i + 1) * HB]
                            last = nc.tensor.matmul(yb[hf, i * HB:(i + 1) * HB], LT[hf, i, hf], rhs, start=True, stop=True)
                    last.then_inc(s["yps_done"], 1)
                    next(fill, None)
                    hold(pe, s["Y_ready"], 7 * n + l + 1)
                    if l == 0:
                        hold(pe, s["X_ready"], 8 * n)
                        nc.tensor.matmul(xb[:, :], idb[:, :], i8[:, :, :].rearrange("p a b -> p (a b)"), start=True, stop=False,
                                         skip_group_check=True)
                        nc.tensor.matmul(xb[:, 0:B * HB], ident, Y[:, :], start=False, stop=False, skip_group_check=True)
                    for i in range(B):
                        for q, hf in enumerate(half):
                            mine = slice(i * HB, (i + 1) * HB)
                            turned = slice((B + i) * HB, (B + i + 1) * HB)
                            if l and (l < LV - 1 or q == 0):
                                nc.tensor.matmul(xb[hf, mine], X[hf, turned], Y[hf, mine], start=False, stop=(l == LV - 1),
                                                 skip_group_check=True)
                            rhs = i64[hf, :] if l == 0 else X[hf, turned]
                            last = nc.tensor.matmul(xb[hf, turned], Y[hf, mine], rhs, start=False, stop=(l == LV - 1),
                                                    skip_group_check=True)
                    last.then_inc(s["xps_done"], 1)
                    next(fill, None)
                hold(pe, s["X_ready"], 8 * n + 8)
                for i in range(B):
                    last = nc.tensor.matmul(yb[HB:P, i * HB:(i + 1) * HB], LT[0:HB, i, HB:P], X[0:HB, i * HB:(i + 1) * HB],
                                            start=True, stop=True)
                last.then_inc(s["yps_done"], 1)
                next(fill, None)
                hold(pe, s["Y_ready"], 7 * n + 7)
                for i in range(B):
                    last = nc.tensor.matmul(yb[0:HB, (B + i) * HB:(B + i + 1) * HB], Y[HB:P, i * HB:(i + 1) * HB], XT[HB:P, i, HB:P],
                                            start=True, stop=True)
                last.then_inc(s["x21_done"], 1)

            def gates(st, pair):
                n = st.n
                if st.c == 0 and pair == 0:
                    pe.wait_ge(s["wg_ready"], st.k + 1)
                if pair == 0:
                    pe.wait_ge(s["W_ready"], B * n + 4)
                else:
                    pe.wait_ge(s["gate_ready"], 2 * n + 1)
                for i in range(2):
                    tile = (2 * pair + i) * CH + st.c
                    terms = [(x, w, k) for x, w in ((hhi, 0), (hhi, 1), (hlo, 0)) for k in range(KC)]
                    for e, (x, w, k) in enumerate(terms):
                        last = nc.tensor.matmul(bank[6][:, i * DV:(i + 1) * DV], x[:, k, tile * P:(tile + 1) * P], wg[w][:, k, :],
                                                start=(e == 0), stop=(e == len(terms) - 1))
                last.then_inc(s["gate_done"], 1)

            def per_pair(st, done, at, waits, lhsT, rhs, rows=P):
                for pair in range(2):
                    for name, value in waits[pair]:
                        pe.wait_ge(s[name], value)
                    for i in range(2):
                        e = 2 * pair + i
                        last = nc.tensor.matmul(bank[at[pair]][0:rows, i * DV:(i + 1) * DV], lhsT(e), rhs(e), start=True, stop=True)
                    last.then_inc(s[done], 1)

            def step(st):
                n, c = st.n, st.c
                fill = iter(())
                if st.project:
                    for part in range(3):
                        projection(st, 0, part)
                    def rest():
                        for t in (1, 2):
                            for part in range(3):
                                yield projection(st, t, part)
                    fill = rest()
                if st.recur:
                    key, qry = kT[st.p], qT[st.p]
                    pe.wait_ge(s["Gm_ready"], n + 1)
                    pe.wait_ge(s["x_added"], B * n + 2)
                    nc.tensor.matmul(bank[5][:, :], cst[:, C_GT:C_GT + P], Gm[:, :, :].rearrange("p b t -> p (b t)"),
                                     start=True, stop=True).then_inc(s["dif_done"], 1)
                    pe.wait_ge(s["kT_ready"], n + 1)
                    pe.wait_ge(s["silu_done"], 3 * n + 3)
                    pe.wait_ge(s["x_added"], B * n + 3)
                    for i in range(B):
                        last = nc.tensor.matmul(bank[6][:, i * P:(i + 1) * P], key[:, i, :], key[:, i, :], start=True, stop=True)
                    last.then_inc(s["gram_done"], 1)
                    pe.wait_ge(s["x_added"], B * n + 4)
                    for i in range(B):
                        last = nc.tensor.matmul(bank[7][:, i * P:(i + 1) * P], key[:, i, :], qry[0:DK, i, :], start=True, stop=True)
                    last.then_inc(s["qk_done"], 1)
                    next(fill, None)
                    per_pair(st, "ks_done", (5, 6), ([("E_ready", n + 1), ("S_ready", B * n + B)], [("LT_ready", n + 1)]),
                             lambda i: key[:, i, :], lambda i: S[:, i, :])
                    next(fill, None)
                    per_pair(st, "qs_done", (7, 5), ([("PT_ready", n + 1)], [("W_ready", B * n + 2)]),
                             lambda i: qry[0:DK, i, :], lambda i: S[:, i, :])
                    levels(st, fill)
                for _ in fill:
                    pass
                if st.recur:
                    gates(st, 0)
                    per_pair(st, "d_done", (7, 5), ([("XT_ready", n + 1), ("W_ready", B * n + 2), ("qs_read", B * n + 2)],
                                                    [("W_ready", B * n + 4), ("qs_read", B * n + 4)]),
                             lambda i: XT[:, i, :], lambda i: W[:, i, :])
                if st.project:
                    to_tokens(st, 0)
                if st.recur:
                    gates(st, 1)
                if st.project:
                    to_tokens(st, 1)
                if st.recur:
                    per_pair(st, "pd_done", (7, 5), ([("D_ready", 2 * n + 1)], [("D_ready", 2 * n + 2)]),
                             lambda i: PT[:, i, :], lambda i: Dl[:, i, :])
                    per_pair(st, "su_done", (6, 7), ([("gate_ready", 2 * n + 2), ("K2_ready", B * n + B)], [("O_ready", 2 * n + 1)]),
                             lambda i: K2[:, i, :], lambda i: Dl[:, i, :], rows=DK)
                if st.project:
                    to_tokens(st, 2)
                    to_tokens(st, 3)
                if st.recur:
                    for hf in range(2):
                        if hf == 0:
                            pe.wait_ge(s["on_ready"], B * n + B)
                            pe.wait_ge(s["O_ready"], 2 * n + 2)
                        else:
                            pe.wait_ge(s["S_ready"], B * n + B + 2)
                        for i in range(B):
                            last = nc.tensor.transpose(bank[5 + hf][0:DK, i * P:(i + 1) * P], on[:, i, hf * DK:(hf + 1) * DK], ident)
                        last.then_inc(s["onT_done"], 1)
                if st.project:
                    keys_back(st)
                if st.recur:
                    if c == 0:
                        pe.wait_ge(s["wo_ready"], st.k + 1)
                    frees = (("S_ready", B * n + 2 * B), ("onT_ready", 2 * n + 1), ("onT_ready", 2 * n + 2), ("x_added", B * n + B + 1))
                    pe.wait_ge(s["onT_ready"], 2 * n + 2)
                    for i in range(B):
                        pe.wait_ge(s[frees[i][0]], frees[i][1])
                        for hf in range(2):
                            last = nc.tensor.matmul(bank[(7, 5, 6, 7)[i]][:, :], onT[:, hf, i, :], wo[:, hf, :], start=(hf == 0), stop=(hf == 1))
                        last.then_inc(s["wo_done"], 1)

            all_steps(pe, step)

        @block.scalar
        def _(a):
            def tap0(st, t):
                q = 3 * st.m + t
                hold(a, s["proj_done"], q + 1)
                if not (isinstance(q, int) and q < 2):
                    hold(a, s["silu_done"], q - 1)
                nc.scalar.activation(y[(st.pm + t) % 2][:, :, :].rearrange("p b t -> p (b t)"), bank[(st.pm + t) % 2][:, :], ACT.Copy,
                                     scale=cw[:, ds(st.ka, 1), t, 3]).then_inc(s["tap0_done"], 1)

            def tanh(st, t):
                q = 3 * st.m + t
                a.wait_ge(s["conv_done"], 7 * q + 7)
                hold(a, s["silu_done"], q)
                nc.scalar.activation(th[:, :, :], y[(st.pm + t) % 2][:, :, :], ACT.Tanh).then_inc(s["tanh_done"], 1)

            def tokens(st, i):
                m = st.m
                a.wait_ge(s["tok_done"], B * m + i + 1)
                if i == 0:
                    a.wait_ge(s["K_ready"], m)
                nc.scalar.activation(tok[:, i, :], bank[2][:, 0:QKV], ACT.Copy).then_inc(s["tok_read"], 1)

            def step(st):
                n, c = st.n, st.c

                def copy_x(l):
                    a.wait_ge(s["xps_done"], LV * n + l + 1)
                    if l < LV - 1:
                        nc.scalar.activation(X[:, :], bank[4][:, :], ACT.Copy).then_inc(s["X_ready"], 1)
                        return
                    nc.scalar.activation(X[0:HB, 0:B * HB], bank[4][0:HB, 0:B * HB], ACT.Copy).then_inc(s["X_ready"], 1)
                    a.wait_ge(s["d_done"], 2 * n)
                    for hf in (slice(0, HB), slice(HB, P)):
                        nc.scalar.activation(XT[hf, :, hf], bank[4][hf, B * HB:].rearrange("p (b t) -> p b t", b=B),
                                             ACT.Copy).then_inc(s["X_ready"], 1)

                def read_qs(pair):
                    a.wait_ge(s["qs_done"], 2 * n + pair + 1)
                    if pair == 0:
                        a.wait_ge(s["onT_done"], 2 * n)
                    for i in (2 * pair, 2 * pair + 1):
                        nc.scalar.activation(Q[:, i, :], bank[(7, 5)[pair]][:, (i % 2) * DV:(i % 2 + 1) * DV], ACT.Copy,
                                             scale=sc[:, EG, ds(n, 1), i]).then_inc(s["qs_read"], 1)

                def gate_tanh(pair):
                    a.wait_ge(s["gate_done"], 2 * n + pair + 1)
                    a.wait_ge(s["gate_ready"], 2 * n + pair)
                    nc.scalar.activation(thg[:, :], bank[6][:, 0:2 * DV], ACT.Tanh, scale=0.5 / SHW).then_inc(s["gtanh_done"], 1)

                def read_d(pair):
                    a.wait_ge(s["d_done"], 2 * n + pair + 1)
                    a.wait_ge(s["su_done"], 2 * n)
                    nc.scalar.activation(Dl[:, 2 * pair:2 * pair + 2, :].rearrange("p b v -> p (b v)"), bank[(7, 5)[pair]][:, 0:2 * DV],
                                         ACT.Copy).then_inc(s["D_ready"], 1)

                if st.project:
                    tap0(st, 0)
                if st.recur:
                    a.wait_ge(s["dif_done"], n + 1)
                    a.wait_ge(s["LT_ready"], n)
                    a.wait_ge(s["K2_ready"], B * n)
                    nc.scalar.activation(E[:, :, :].rearrange("p b t -> p (b t)"), bank[5][:, :], ACT.Exp).then_inc(s["E_ready"], 1)
                if st.project:
                    tanh(st, 0)
                if st.recur:
                    read_qs(0)
                if st.project:
                    tap0(st, 1)
                if st.recur:
                    read_qs(1)
                    copy_x(0)
                    copy_x(1)
                if st.project:
                    tanh(st, 1)
                    tap0(st, 2)
                if st.recur:
                    copy_x(2)
                    copy_x(3)
                if st.project:
                    tanh(st, 2)
                if st.recur:
                    copy_x(4)
                    copy_x(5)
                    gate_tanh(0)
                    read_d(0)
                    read_d(1)
                if st.project:
                    tokens(st, 0)
                if st.recur:
                    gate_tanh(1)
                if st.project:
                    tokens(st, 1)
                    tokens(st, 2)
                    tokens(st, 3)
                if st.recur:
                    for i in range(B):
                        if i % 2 == 0:
                            a.wait_ge(s["O_ready"], 2 * n + i // 2 + 1)
                        if i == 0:
                            a.wait_ge(s["ssq_done"], B * n)
                            a.wait_ge(s["r_ready"], 3 * n)
                        nc.scalar.activation(junk[:, i, :], O[:, i, :], ACT.Square, accum_out=sso[:, i:i + 1]).then_inc(s["ssq_done"], 1)
                    for hf in range(2):
                        a.wait_ge(s["onT_done"], 2 * n + hf + 1)
                        a.wait_ge(s["wo_done"], B * n)
                        nc.scalar.activation(onT[:, hf, :, :].rearrange("p b t -> p (b t)"), bank[5 + hf][0:DK, :], ACT.Copy).then_inc(s["onT_ready"], 1)
                if st.project:
                    m = st.m
                    a.wait_ge(s["kT_done"], m + 1)
                    nc.scalar.activation(kT[st.pm][:, :, :].rearrange("p b t -> p (b t)"), bank[2][0:DK, :], ACT.Copy).then_inc(s["kT_ready"], 1)

            a.wait_ge(s["cw_ready"], 2)
            all_steps(a, step)

        @block.vector
        def _(v):
            def conv(st, t, tap):
                q = 3 * st.m + t
                if tap == 1:
                    v.wait_ge(s["tap0_done"], q + 1)
                else:
                    v.wait_ge(s["conv_done"], 7 * q + tap - 1)
                yy, pp = y[(st.pm + t) % 2], bank[(st.pm + t) % 2][:, :].rearrange("p (b t) -> p b t", b=B)
                nc.vector.scalar_tensor_tensor(out=yy[:, :, tap:], in0=pp[:, :, 0:P - tap], scalar=cw[:, ds(st.ka, 1), t, 3 - tap],
                                               in1=yy[:, :, tap:], op0=ALU.mult, op1=ALU.add).then_inc(s["conv_done"], 1)
                if tap < 3:
                    return
                if st.cm:
                    old = tail[st.p][:, t, :, :]
                    for back in (1, 2, 3):
                        v.wait_ge(s["conv_done"], 7 * q + 2 + back)
                        nc.vector.scalar_tensor_tensor(out=yy[:, :, 0:back], in0=old[:, :, 3 - back:], scalar=cw[:, ds(st.ka, 1), t, 3 - back],
                                                       in1=yy[:, :, 0:back], op0=ALU.mult, op1=ALU.add).then_inc(s["conv_done"], 1)
                nc.vector.tensor_copy(tail[st.pm][:, t, :, :], pp[:, :, P - 3:]).then_inc(s["conv_done"], 1 if st.cm else 4)

            def silu(st, t):
                q = 3 * st.m + t
                v.wait_ge(s["tanh_done"], q + 1)
                v.wait_ge(s["conv_done"], 7 * q + 7)
                if t == 0:
                    if st.recur:
                        v.wait_ge(s["qs_done"], 2 * st.n)
                    dst = qT[st.pm][:, :, :]
                else:
                    v.wait_ge(s["tok_done"], B * st.m)
                    dst = yv[:, t - 1, :, :]
                nc.vector.scalar_tensor_tensor(out=dst, in0=th[:, :, :], scalar=1.0, in1=y[(st.pm + t) % 2][:, :, :],
                                               op0=ALU.add, op1=ALU.mult).then_inc(s["silu_done"], 1)

            def step(st):
                n, m, c = st.n, st.m, st.c

                def level(l):
                    rows = slice(0, P) if l < LV else slice(HB, P)
                    v.wait_ge(s["yps_done"], 7 * n + l + 1)
                    if l == 0:
                        v.wait_ge(s["nbM_ready"], n + 1)
                    nc.vector.tensor_tensor(Y[rows, :], bank[3][rows, 0:B * HB], nbM[rows, l, :, :].rearrange("p b t -> p (b t)"),
                                            ALU.mult).then_inc(s["Y_ready"], 1)

                def w_pair(pair):
                    v.wait_ge(s["ks_done"], 2 * n + pair + 1)
                    if pair == 0:
                        v.wait_ge(s["on_ready"], B * n)
                        v.wait_ge(s["ssq_done"], B * n)
                        v.wait_ge(s["V_ready"], n + 1)
                    for i in (2 * pair, 2 * pair + 1):
                        nc.vector.scalar_tensor_tensor(out=W[:, i, :], in0=bank[5 + pair][:, (i % 2) * DV:(i % 2 + 1) * DV],
                                                       scalar=sc[:, NBEG, ds(n, 1), i], in1=V[st.p][:, i, :],
                                                       op0=ALU.mult, op1=ALU.add).then_inc(s["W_ready"], 1)

                def gate_pair(pair):
                    v.wait_ge(s["gtanh_done"], 2 * n + pair + 1)
                    if pair == 0:
                        v.wait_ge(s["on_ready"], B * n)
                    nc.vector.scalar_tensor_tensor(out=gate[:, 2 * pair:2 * pair + 2, :].rearrange("p b v -> p (b v)"), in0=thg[:, :],
                                                   scalar=1.0, in1=bank[6][:, 0:2 * DV], op0=ALU.add, op1=ALU.mult).then_inc(s["gate_ready"], 1)

                def out_pair(pair):
                    v.wait_ge(s["pd_done"], 2 * n + pair + 1)
                    v.wait_ge(s["qs_read"], B * n + 2 * pair + 2)
                    two = slice(2 * pair, 2 * pair + 2)
                    nc.vector.tensor_tensor(O[:, two, :].rearrange("p b v -> p (b v)"), bank[(7, 5)[pair]][:, 0:2 * DV],
                                            Q[:, two, :].rearrange("p b v -> p (b v)"), ALU.add).then_inc(s["O_ready"], 1)

                if st.project:
                    for tap in (1, 2, 3):
                        conv(st, 0, tap)
                if st.recur:
                    v.wait_ge(s["E_ready"], n + 1)
                    v.wait_ge(s["gram_done"], n + 1)
                    v.wait_ge(s["yps_done"], 7 * n)
                    nc.vector.tensor_tensor(LT[:, :, :].rearrange("p b t -> p (b t)"), bank[6][:, :],
                                            E[:, :, :].rearrange("p b t -> p (b t)"), ALU.mult).then_inc(s["LT_ready"], 1)
                    v.wait_ge(s["Em_ready"], n + 1)
                    v.wait_ge(s["qk_done"], n + 1)
                    v.wait_ge(s["pd_done"], 2 * n)
                    nc.vector.tensor_tensor(PT[:, :, :].rearrange("p b t -> p (b t)"), bank[7][:, :],
                                            Em[:, :, :].rearrange("p b t -> p (b t)"), ALU.mult).then_inc(s["PT_ready"], 1)
                    w_pair(0)
                if st.project:
                    silu(st, 0)
                if st.recur:
                    w_pair(1)
                    level(0)
                if st.project:
                    conv(st, 1, 1)
                    conv(st, 1, 2)
                if st.recur:
                    level(1)
                if st.project:
                    conv(st, 1, 3)
                if st.recur:
                    level(2)
                if st.project:
                    silu(st, 1)
                if st.recur:
                    level(3)
                if st.project:
                    conv(st, 2, 1)
                    conv(st, 2, 2)
                if st.recur:
                    level(4)
                if st.project:
                    conv(st, 2, 3)
                if st.recur:
                    level(5)
                if st.project:
                    silu(st, 2)
                if st.recur:
                    level(6)
                    v.wait_ge(s["x21_done"], n + 1)
                    nc.vector.tensor_copy(XT[0:HB, :, HB:P], bank[3][0:HB, B * HB:].rearrange("p (b t) -> p b t", b=B)).then_inc(s["XT_ready"], 1)
                    gate_pair(0)
                    gate_pair(1)
                    out_pair(0)
                    out_pair(1)
                    for i in range(B):
                        if i % 2 == 0:
                            v.wait_ge(s["su_done"], 2 * n + i // 2 + 1)
                        if c < CH - 1:
                            nc.vector.scalar_tensor_tensor(out=S[:, i, :], in0=S[:, i, :], scalar=dec[0:DK, ds(n, 1), i],
                                                           in1=bank[6 + i // 2][0:DK, (i % 2) * DV:(i % 2 + 1) * DV],
                                                           op0=ALU.mult, op1=ALU.add).then_inc(s["S_ready"], 1)
                        elif i % 2 == 1:
                            nc.vector.memset(S[:, i - 1:i + 1, :], 0.0).then_inc(s["S_ready"], 2)
                if st.project:
                    v.wait_ge(s["sq_done"], m + 1)
                    v.wait_ge(s["kappa_done"], 3 * m)
                    nc.vector.tensor_reduce(ss[:, :, :], sq[:, :, :, :], AXX, ALU.add).then_inc(s["ss_done"], 1)
                if st.recur:
                    v.wait_ge(s["r_ready"], 3 * n + 3)
                    v.wait_ge(s["O_ready"], 2 * n + 2)
                    v.wait_ge(s["gate_ready"], 2 * n + 2)
                    for i in range(B):
                        nc.vector.scalar_tensor_tensor(out=on[:, i, :], in0=O[:, i, :], scalar=rn[:, i:i + 1], in1=gate[:, i, :],
                                                       op0=ALU.mult, op1=ALU.mult).then_inc(s["on_ready"], 1)
                    for i in range(B):
                        v.wait_ge(s["wo_done"], B * n + i + 1)
                        xs = x_sb[:, i * CH + c, :]
                        nc.vector.tensor_tensor(xs, xs, bank[(7, 5, 6, 7)[i]][:, :], ALU.add).then_inc(s["x_added"], 1)

            nc.vector.memset(S[:, :, :], 0.0).then_inc(s["S_ready"], B)
            nc.vector.memset(ss[:, :, :], 0.0).then_inc(s["x_added"], B)
            v.wait_ge(s["x_added"], B)
            v.wait_ge(s["cw_ready"], 2)
            all_steps(v, step)


def stage_sets(nc, io, keep):
    x_sb, cst, bank = keep["x"], keep["cst"], keep["bank"]
    with ExitStack() as ctx:
        def sb(name, shape, dt=F32):
            return ctx.enter_context(nc.sbuf_tensor("s_" + name, shape, dt))

        def sem(name):
            return ctx.enter_context(nc.semaphore("s_" + name))

        R = sb("R", [NSET, D])
        RT = sb("RT", [P, KC, NSET])
        Wq = sb("Wq", [P, KC, D])
        M = sb("M", [P, KC, NSET])
        bq = sb("bq", [P, KC])
        crow = sb("crow", [1, NSET])
        one = sb("one", [1, P])
        itok = sb("itok", [P, CH, TOPK_IN], I32)
        itf = sb("itf", [P, CH, TOPK_IN])
        bias = sb("bias", [P, CH, NSET])
        ctxs = sb("ctxs", [NSET, B, D])
        stats = sb("stats", [P, 6])
        mv = sb("mv", [P, NT, 2])
        var = sb("var", [P, NT])
        half = sb("half", [P, NT])
        rstd = sb("rstd", [P, NT])
        hn = [sb(f"hn{p}", [P, D]) for p in range(2)]
        hT = [sb(f"hT{p}", [P, KC, P]) for p in range(2)]
        score = sb("score", [P, NT, NSET])
        top = sb("top", [P, NT, 8])
        topi = sb("topi", [P, NT, 8], U32)
        idx = sb("idx", [P, NT, 2])
        gap = sb("gap", [P, NT])
        eg = sb("eg", [P, NT])
        den = sb("den", [P, NT])
        w0 = sb("w0", [P, NT])
        w1 = sb("w1", [P, NT])
        wt = sb("wt", [P, NT, NSET])
        wt1 = sb("wt1", [P, NT, NSET])
        wT = [sb(f"wT{p}", [NSET, P]) for p in range(2)]
        par_in = sem("par_in")
        small = sem("small")
        vs = sem("vs")
        vlink = sem("vlink")
        stat = sem("stat")
        rstd_ready = sem("rstd_ready")
        r_done = sem("r_done")
        rT_ready = sem("rT_ready")
        m_done = sem("m_done")
        M_ready = sem("M_ready")
        bias_ready = sem("bias_ready")
        hn_ready = [sem(f"hn_ready{p}") for p in range(2)]
        hT_done = [sem(f"hT_done{p}") for p in range(2)]
        hT_ready = [sem(f"hT_ready{p}") for p in range(2)]
        sc_done = [sem(f"sc_done{p}") for p in range(2)]
        score_ready = [sem(f"score_ready{p}") for p in range(2)]
        eg_ready = sem("eg_ready")
        wt_ready = sem("wt_ready")
        wT_done = [sem(f"wT_done{p}") for p in range(2)]
        wT_ready = [sem(f"wT_ready{p}") for p in range(2)]
        o_done = [sem(f"o_done{p}") for p in range(2)]
        added = [sem(f"added{p}") for p in range(2)]
        block = ctx.enter_context(nc.Block())
        ident = cst[:, C_ID:C_ID + P]
        iota = cst[:, C_IOTA:C_IOTA + NSET]

        @block.sync
        def _(sp):
            sp.dma_start(R[:, :], io["L0_xattn_desc_router"]).then_inc(par_in, 16)
            sp.dma_start(Wq[:, :, :], io["L0_xattn_W_q"].rearrange("(k p) d -> p k d", p=P)).then_inc(par_in, 16)
            sp.dma_start(bq[:, :], io["L0_xattn_b_q"].rearrange("(k p) -> p k", p=P), allow_slow_non_contiguous=True).then_inc(par_in, 16)
            sp.dma_start(itok[:, :, :], io["itok_Sx4_0_63"].rearrange("(c p) k -> p c k", p=P)).then_inc(par_in, 16)
            sp.dma_start(ctxs[:, :, :], io["ctx_2048"].rearrange("b n d -> n b d")).then_inc(par_in, 16)

        @block.gpsimd
        def _(pool):
            nc.gpsimd.memset(half[:, :], -0.5).then_inc(small, 1)
            nc.gpsimd.memset(one[:, :], 1.0).then_inc(small, 1)
            pool.wait_ge(stat, 2 * NT)
            nc.gpsimd.tensor_scalar(var[:, :], mv[:, :, 1], LN_EPS, None, ALU.add).then_inc(small, 1)
            pool.wait_ge(small, 3)
            nc.gpsimd.tensor_tensor(rstd[:, :], var[:, :], half[:, :], ALU.pow).then_inc(rstd_ready, 1)

        @block.tensor
        def _(pe):
            pe.wait_ge(par_in, 80)
            for k in range(KC):
                last = nc.tensor.transpose(bank[0][:, k * NSET:(k + 1) * NSET], R[:, k * P:(k + 1) * P], ident[0:NSET, 0:NSET])
            last.then_inc(r_done, 1)
            pe.wait_ge(rT_ready, 1)
            for d in range(KC):
                for e in range(KC):
                    last = nc.tensor.matmul(bank[1][:, d * NSET:(d + 1) * NSET], Wq[:, e, d * P:(d + 1) * P], RT[:, e, :],
                                            start=(e == 0), stop=(e == KC - 1))
            for e in range(KC):
                last = nc.tensor.matmul(bank[1][0:1, KC * NSET:(KC + 1) * NSET], bq[:, e:e + 1], RT[:, e, :],
                                        start=(e == 0), stop=(e == KC - 1))
            last.then_inc(m_done, 1)
            pe.wait_ge(M_ready, 2)
            pe.wait_ge(small, 2)
            def pair(i):
                for p in range(2):
                    pe.wait_ge(hn_ready[p], i + 1)
                    pe.wait_ge(hT_ready[p], i)
                    for k in range(KC):
                        last = nc.tensor.transpose(bank[2 + p][:, k * P:(k + 1) * P], hn[p][:, k * P:(k + 1) * P], ident)
                    last.then_inc(hT_done[p], 1)
                for p in range(2):
                    pe.wait_ge(hT_ready[p], i + 1)
                    pe.wait_ge(score_ready[p], i)
                    for k in range(KC):
                        nc.tensor.matmul(bank[4 + p][:, 0:NSET], hT[p][:, k, :], M[:, k, :], start=(k == 0), stop=False)
                    nc.tensor.matmul(bank[4 + p][:, 0:NSET], one[0:1, :], crow[0:1, :], start=False, stop=True).then_inc(sc_done[p], 1)

            tile_pairs(pe, pair)
            pe.wait_ge(wt_ready, 1)
            for t in range(NT):
                p, i = t % 2, t // 2
                if i:
                    pe.wait_ge(wT_ready[p], i)
                nc.tensor.transpose(bank[6 + p][0:NSET, 0:P], wt[:, t, :], ident).then_inc(wT_done[p], 1)
                pe.wait_ge(wT_ready[p], i + 1)
                if i:
                    pe.wait_ge(added[p], i)
                nc.tensor.matmul(bank[p][:, :], wT[p][:, :], ctxs[:, t // CH, :], start=True, stop=True).then_inc(o_done[p], 1)

        @block.scalar
        def _(a):
            a.wait_ge(r_done, 1)
            nc.scalar.activation(RT[:, :, :].rearrange("p k n -> p (k n)"), bank[0][:, 0:KC * NSET], ACT.Copy).then_inc(rT_ready, 1)
            a.wait_ge(m_done, 1)
            nc.scalar.activation(M[:, :, :].rearrange("p k n -> p (k n)"), bank[1][:, 0:KC * NSET], ACT.Copy, scale=float(D) ** -0.5).then_inc(M_ready, 1)
            nc.scalar.activation(crow[:, :], bank[1][0:1, KC * NSET:(KC + 1) * NSET], ACT.Copy, scale=float(D) ** -0.5).then_inc(M_ready, 1)
            def pair(i):
                for p in range(2):
                    a.wait_ge(hT_done[p], i + 1)
                    a.wait_ge(sc_done[p], i)
                    nc.scalar.activation(hT[p][:, :, :].rearrange("p k t -> p (k t)"), bank[2 + p][:, :], ACT.Copy).then_inc(hT_ready[p], 1)

            tile_pairs(a, pair)
            a.wait_ge(vs, 1)
            nc.scalar.activation(eg[:, :], gap[:, :], ACT.Exp).then_inc(eg_ready, 1)
            for t in range(NT):
                p, i = t % 2, t // 2
                a.wait_ge(wT_done[p], i + 1)
                if i:
                    a.wait_ge(o_done[p], i)
                nc.scalar.activation(wT[p][:, :], bank[6 + p][0:NSET, 0:P], ACT.Copy).then_inc(wT_ready[p], 1)

        @block.vector
        def _(v):
            for t in range(NT):
                if t:
                    v.wait_ge(stat, 2 * t)
                nc.vector.bn_stats(stats[:, :], x_sb[:, t, :]).then_inc(stat, 1)
                v.wait_ge(stat, 2 * t + 1)
                nc.vector.bn_aggr(mv[:, t, :], stats[:, :]).then_inc(stat, 1)
            v.wait_ge(par_in, 80)
            nc.vector.tensor_copy(itf[:, :, :], itok[:, :, :]).then_inc(bias_ready, 1)
            for c in range(CH):
                for k in range(TOPK_IN):
                    v.wait_ge(bias_ready, 1 + c * 5 + k)
                    if k == 0:
                        nc.vector.tensor_scalar(bias[:, c, :], iota, itf[:, c, 0:1], None, ALU.is_equal).then_inc(bias_ready, 1)
                    else:
                        nc.vector.scalar_tensor_tensor(out=bias[:, c, :], in0=iota, scalar=itf[:, c, k:k + 1], in1=bias[:, c, :],
                                                       op0=ALU.is_equal, op1=ALU.max).then_inc(bias_ready, 1)
                v.wait_ge(bias_ready, 1 + c * 5 + 4)
                nc.vector.tensor_scalar(bias[:, c, :], bias[:, c, :], 1e30, -1e30, ALU.mult, ALU.add).then_inc(bias_ready, 1)
            v.wait_ge(rstd_ready, 1)
            v.wait_ge(stat, 2 * NT)
            v.wait_ge(bias_ready, 1 + 5 * CH)
            def pair(i):
                for p in range(2):
                    v.wait_ge(hT_done[p], i)
                    nc.vector.tensor_scalar(hn[p][:, :], x_sb[:, ds(i * 2 + p, 1), :].squeeze(1), mv[:, ds(i * 2 + p, 1), 0],
                                            rstd[:, ds(i * 2 + p, 1)], ALU.subtract, ALU.mult).then_inc(hn_ready[p], 1)
                for p in range(2):
                    v.wait_ge(sc_done[p], i + 1)
                    nc.vector.tensor_copy(score[:, ds(i * 2 + p, 1), :].squeeze(1), bank[4 + p][:, 0:NSET]).then_inc(score_ready[p], 1)

            tile_pairs(v, pair)
            for p in range(2):
                v.wait_ge(score_ready[p], NT // 2)
            nc.vector.tensor_tensor(score[:, :, :].rearrange("p (b c) n -> p b (c n)", b=B), score[:, :, :].rearrange("p (b c) n -> p b (c n)", b=B),
                                    over(bias[:, :, :].rearrange("p c n -> p (c n)"), 1, B), ALU.add).then_inc(vlink, 1)
            v.wait_ge(vlink, 1)
            link = chain(v, vlink, 1)
            link(nc.vector.memset(den[:, :], 0.0))
            for t in range(NT):
                link(nc.vector.max(top[:, t, :], score[:, t, :]))
                link(nc.vector.max_index(topi[:, t, :], top[:, t, :], score[:, t, :]))
            link(nc.vector.tensor_copy(idx[:, :, :], topi[:, :, 0:2]))
            nc.vector.tensor_tensor(gap[:, :], top[:, :, 1], top[:, :, 0], ALU.subtract).then_inc(vs, 1)
            v.wait_ge(eg_ready, 1)
            link(nc.vector.tensor_scalar(den[:, :], eg[:, :], 1.0, None, ALU.add))
            link(nc.vector.reciprocal(w0[:, :], den[:, :]))
            link(nc.vector.tensor_tensor(w1[:, :], eg[:, :], w0[:, :], ALU.mult))
            for w, k, wk in ((wt, 0, w0), (wt1, 1, w1)):
                link(nc.vector.tensor_tensor(w[:, :, :], over(iota, 1, NT), over(idx[:, :, k], 2, NSET), ALU.is_equal))
                link(nc.vector.tensor_tensor(w[:, :, :], w[:, :, :], over(wk[:, :], 2, NSET), ALU.mult))
            nc.vector.tensor_tensor(wt[:, :, :], wt[:, :, :], wt1[:, :, :], ALU.add).then_inc(wt_ready, 1)
            for t in range(NT):
                p, i = t % 2, t // 2
                v.wait_ge(o_done[p], i + 1)
                nc.vector.tensor_tensor(x_sb[:, t, :], x_sb[:, t, :], bank[p][:, :], ALU.add).then_inc(added[p], 1)


def chain(eng, sem, start=0):
    count = [start]

    def link(ins):
        count[0] += 1
        ins.then_inc(sem, 1)
        eng.wait_ge(sem, count[0])

    return link


def stage_ffn(nc, io, keep):
    x_sb, cst, bank = keep["x"], keep["cst"], keep["bank"]
    NH, FB = FF // P, FF // 512
    with ExitStack() as ctx:
        def sb(name, shape, dt=F32):
            return ctx.enter_context(nc.sbuf_tensor("f_" + name, shape, dt))

        def sem(name):
            return ctx.enter_context(nc.semaphore("f_" + name))

        NQ = 4
        st = [sb(f"st{q}", [P, NQ, D]) for q in range(NQ)]
        rnd = sb("rnd", [P, NQ, D])
        tern = [sb(f"tern{q}", [P, NQ, D], BF16) for q in range(2)]
        wgT = sb("wgT", [P, KC, FF], BF16)
        wvT = sb("wvT", [P, KC, FF], BF16)
        woT = sb("woT", [P, NH, D], BF16)
        idb = sb("idb", [P, P], BF16)
        onesm = sb("onesm", [P, P])
        asum = sb("asum", [P, 3, NQ])
        asum1 = sb("asum1", [P, 3])
        gam = sb("gam", [P, 3])
        rgam = sb("rgam", [P, 3])
        gb = sb("gb", [P, FF])
        vb = sb("vb", [P, FF])
        ob = sb("ob", [P, D])
        stats = sb("stats", [P, 6])
        mv = sb("mv", [P, NT, 2])
        var = sb("var", [P, NT])
        half = sb("half", [P, NT])
        rstd = sb("rstd", [P, NT])
        hn = sb("hn", [P, D])
        hr = sb("hr", [P, D])
        hq = sb("hq", [P, D], BF16)
        hqT = [sb(f"hqT{p}", [P, KC, P], BF16) for p in range(2)]
        g4 = [sb(f"g4{p}", [P, 4]) for p in range(2)]
        fs = [sb(f"fs{p}", [P, 2]) for p in range(2)]
        zg = sb("zg", [P, FF])
        zv = sb("zv", [P, FF])
        aq = sb("aq", [P, FF], BF16)
        aqT = sb("aqT", [P, NH, P], BF16)
        a4 = sb("a4", [P, 4])
        fo = sb("fo", [P, 1])
        outt = [sb(f"outt{p}", [P, D]) for p in range(2)]

        names = """par_in gsmall stat rstd_ready asum_ready gsum_done gam_ready vw rnd_ready tern_ready wT_done wT_ready
            v_chain hq_ready hqT_done hqT_ready fs_ready gate_done val_done zg_ready silu_ready zv_ready
            aq_ready aqT_done aqT_ready fo_ready vl out_done out_ready stored""".split()
        s = {name: sem(name) for name in names}
        st_in = [sem(f"st_in{q}") for q in range(NQ)]
        block = ctx.enter_context(nc.Block())
        srcs = [io["L0_ffn_gate_w"].rearrange("(k p) d -> p k d", p=P), io["L0_ffn_val_w"].rearrange("(k p) d -> p k d", p=P),
                io["L0_ffn_out_w"].rearrange("(k p) (q d) -> p q k d", p=P, q=NQ)]

        @block.sync
        def _(sp):
            for w in range(3):
                for q in range(NQ):
                    if w:
                        sp.wait_ge(s["rnd_ready"], (w - 1) * NQ + q + 1)
                    src = srcs[w][:, q * NQ:(q + 1) * NQ, :] if w < 2 else srcs[w][:, q]
                    sp.dma_start(st[q][:, :, :], src).then_inc(st_in[q], 16)
                if w == 0:
                    sp.dma_start(gb[:, :], io["L0_ffn_gate_b"].partition_broadcast(P)).then_inc(s["par_in"], 16)
                    sp.dma_start(vb[:, :], io["L0_ffn_val_b"].partition_broadcast(P)).then_inc(s["par_in"], 16)
                    sp.dma_start(ob[:, :], io["L0_ffn_out_b"].partition_broadcast(P)).then_inc(s["par_in"], 16)
            def pair(i):
                for p in range(2):
                    sp.wait_ge(s["out_ready"], i * 2 + p + 1)
                    row = (i * 2 + p) * P
                    sp.dma_start(io["out"].rearrange("b t d -> (b t) d")[ds(row, P), :], outt[p][:, :]).then_inc(s["stored"], 16)

            tile_pairs(sp, pair)
            sp.wait_ge(s["stored"], 16 * NT)

        @block.gpsimd
        def _(pool):
            nc.gpsimd.memset(half[:, :], -0.5).then_inc(s["gsmall"], 1)
            nc.gpsimd.memset(onesm[:, :], 1.0 / (FF * D)).then_inc(s["gsmall"], 1)
            nc.gpsimd.tensor_copy(idb[:, :], cst[:, C_ID:C_ID + P]).then_inc(s["gsmall"], 1)
            pool.wait_ge(s["stat"], 2 * NT)
            nc.gpsimd.tensor_scalar(var[:, :], mv[:, :, 1], LN_EPS, None, ALU.add).then_inc(s["gsmall"], 1)
            pool.wait_ge(s["gsmall"], 4)
            nc.gpsimd.tensor_tensor(rstd[:, :], var[:, :], half[:, :], ALU.pow).then_inc(s["rstd_ready"], 1)

        @block.scalar
        def _(a):
            for w in range(3):
                for q in range(NQ):
                    e = w * NQ + q
                    if q == 0:
                        a.wait_ge(s["gam_ready"], w + 1)
                    if e:
                        a.wait_ge(s["tern_ready"], e)
                    nc.scalar.activation(rnd[:, :, :], st[q][:, :, :], ACT.Copy, scale=rgam[:, w:w + 1], bias=ROUND).then_inc(s["rnd_ready"], 1)
                    for k in range(NQ):
                        a.wait_ge(s["wT_done"], e * NQ + k + 1)
                        pt = bank[2 + k][:, :].bitcast(BF16)[:, 0:D].rearrange("p (k t) -> p k t", k=KC)
                        if w < 2:
                            dst = (wgT, wvT)[w][:, :, (q * NQ + k) * P:(q * NQ + k + 1) * P]
                        else:
                            dst = woT[:, q * NQ:(q + 1) * NQ, k * P:(k + 1) * P]
                        nc.scalar.activation(dst, pt, ACT.Copy).then_inc(s["wT_ready"], 1)
            def pair(i):
                for p in range(2):
                    t = i * 2 + p
                    a.wait_ge(s["hqT_done"], t + 1)
                    nc.scalar.activation(hqT[p][:, :, :].rearrange("p k t -> p (k t)"), bank[7][:, :].bitcast(BF16)[:, 0:D], ACT.Copy).then_inc(s["hqT_ready"], 1)
                    for f in range(FB):
                        a.wait_ge(s["zg_ready"], t * FB + f + 1)
                        nc.scalar.activation(zg[:, f * 512:(f + 1) * 512], zg[:, f * 512:(f + 1) * 512], ACT.Silu).then_inc(s["silu_ready"], 1)
                    for f in range(2):
                        a.wait_ge(s["aqT_done"], t * 2 + f + 1)
                        nc.scalar.activation(aqT[:, f * 8:(f + 1) * 8, :].rearrange("p k t -> p (k t)"), bank[6][:, :].bitcast(BF16), ACT.Copy)\
                            .then_inc(s["aqT_ready"], 1)

            tile_pairs(a, pair)

        @block.tensor
        def _(pe):
            pe.wait_ge(s["gsmall"], 3)
            for w in range(3):
                pe.wait_ge(s["asum_ready"], w + 1)
                nc.tensor.matmul(bank[0][:, w:w + 1], onesm[:, :], asum1[:, w:w + 1], start=True, stop=True).then_inc(s["gsum_done"], 1)
                for q in range(NQ):
                    e = w * NQ + q
                    pe.wait_ge(s["tern_ready"], e + 1)
                    for k in range(NQ):
                        if e:
                            pe.wait_ge(s["wT_ready"], (e - 1) * NQ + k + 1)
                        for d in range(KC):
                            last = nc.tensor.transpose(bank[2 + k][:, :].bitcast(BF16)[:, d * P:(d + 1) * P], tern[e % 2][:, k, d * P:(d + 1) * P], idb[:, :])
                        last.then_inc(s["wT_done"], 1)
            pe.wait_ge(s["wT_ready"], 3 * NQ * NQ)
            def pair(i):
                for p in range(2):
                    t = i * 2 + p
                    pe.wait_ge(s["hq_ready"], t + 1)
                    pe.wait_ge(s["hqT_ready"], t)
                    for k in range(KC):
                        last = nc.tensor.transpose(bank[7][:, :].bitcast(BF16)[:, k * P:(k + 1) * P], hq[:, k * P:(k + 1) * P], idb[:, :])
                    last.then_inc(s["hqT_done"], 1)
                    pe.wait_ge(s["hqT_ready"], t + 1)
                    for f in range(FB):
                        fs_ = slice(f * 512, (f + 1) * 512)
                        for wT, b0, done, read in ((wgT, 0, "gate_done", "zg_ready"), (wvT, 2, "val_done", "zv_ready")):
                            acc = bank[b0 + f % 2]
                            if f >= 2:
                                pe.wait_ge(s[read], t * FB + f - 1)
                            else:
                                pe.wait_ge(s[read], t * FB)
                            for k in range(KC):
                                last = nc.tensor.matmul(acc[:, :], hqT[p][:, k, :], wT[:, k, fs_], start=(k == 0), stop=(k == KC - 1))
                            last.then_inc(s[done], 1)
                    for f in range(2):
                        if f == 0:
                            pe.wait_ge(s["aq_ready"], t + 1)
                        pe.wait_ge(s["aqT_ready"], t * 2 + f)
                        for k in range(8):
                            last = nc.tensor.transpose(bank[6][:, :].bitcast(BF16)[:, k * P:(k + 1) * P], aq[:, (f * 8 + k) * P:(f * 8 + k + 1) * P], idb[:, :])
                        last.then_inc(s["aqT_done"], 1)
                    pe.wait_ge(s["aqT_ready"], t * 2 + 2)
                    pe.wait_ge(s["out_ready"], t)
                    for k in range(NH):
                        last = nc.tensor.matmul(bank[5][:, :], aqT[:, k, :], woT[:, k, :], start=(k == 0), stop=(k == NH - 1))
                    last.then_inc(s["out_done"], 1)

            tile_pairs(pe, pair)

        @block.vector
        def _(v):
            for t in range(NT):
                if t:
                    v.wait_ge(s["stat"], 2 * t)
                nc.vector.bn_stats(stats[:, :], x_sb[:, t, :]).then_inc(s["stat"], 1)
                v.wait_ge(s["stat"], 2 * t + 1)
                nc.vector.bn_aggr(mv[:, t, :], stats[:, :]).then_inc(s["stat"], 1)
            for w in range(3):
                for q in range(NQ):
                    v.wait_ge(st_in[q], 16 * (w + 1))
                    nc.vector.tensor_reduce(asum[:, w, q:q + 1], st[q][:, :, :].rearrange("p k d -> p (k d)"), AXX, ALU.add,
                                            apply_absolute_value=True).then_inc(s["vw"], 1)
                v.wait_ge(s["vw"], 7 * w + 4)
                nc.vector.tensor_reduce(asum1[:, w:w + 1], asum[:, w, :], AXX, ALU.add).then_inc(s["asum_ready"], 1)
                v.wait_ge(s["gsum_done"], w + 1)
                nc.vector.tensor_scalar(gam[:, w:w + 1], bank[0][:, w:w + 1], 1e-5, None, ALU.max).then_inc(s["vw"], 1)
                v.wait_ge(s["vw"], 7 * w + 5)
                nc.vector.reciprocal(rgam[:, w:w + 1], gam[:, w:w + 1]).then_inc(s["gam_ready"], 1)
                for q in range(NQ):
                    e = w * NQ + q
                    v.wait_ge(s["rnd_ready"], e + 1)
                    nc.vector.tensor_scalar(rnd[:, :, :], rnd[:, :, :], ROUND, 1.0, ALU.subtract, ALU.min).then_inc(s["v_chain"], 1)
                    v.wait_ge(s["v_chain"], e + 1)
                    if e >= 2:
                        v.wait_ge(s["wT_done"], (e - 1) * NQ)
                    nc.vector.tensor_scalar(tern[e % 2][:, :, :], rnd[:, :, :], -1.0, None, ALU.max).then_inc(s["tern_ready"], 1)
                v.wait_ge(s["tern_ready"], (w + 1) * NQ)
                nc.vector.memset(hr[:, 0:1], 0.0).then_inc(s["vw"], 2)
            v.wait_ge(s["rstd_ready"], 1)
            v.wait_ge(s["stat"], 2 * NT)
            v.wait_ge(s["vw"], 21)
            v.wait_ge(s["gam_ready"], 3)
            v.wait_ge(s["par_in"], 48)
            def pair(i):
                for p in range(2):
                    t = i * 2 + p
                    base, count = t * 15, [0]

                    def link(ins):
                        count[0] += 1
                        ins.then_inc(s["vl"], 1)
                        v.wait_ge(s["vl"], base + count[0])

                    xt = x_sb[:, ds(t, 1), :].squeeze(1)
                    link(nc.vector.tensor_scalar(hn[:, :], xt, mv[:, ds(t, 1), 0], rstd[:, ds(t, 1)], ALU.subtract, ALU.mult))
                    link(nc.vector.tensor_reduce(g4[p][:, 0:1], hn[:, :], AXX, ALU.max, apply_absolute_value=True))
                    link(nc.vector.tensor_scalar(g4[p][:, 0:1], g4[p][:, 0:1], 1e-5, None, ALU.max))
                    link(nc.vector.reciprocal(g4[p][:, 1:2], g4[p][:, 0:1]))
                    link(nc.vector.tensor_scalar(g4[p][:, 2:3], g4[p][:, 1:2], 127.0, None, ALU.mult))
                    link(nc.vector.tensor_scalar(hr[:, :], hn[:, :], g4[p][:, 2:3], ROUND, ALU.mult, ALU.add))
                    v.wait_ge(s["hqT_done"], t)
                    nc.vector.tensor_scalar(hq[:, :], hr[:, :], ROUND, 127.0, ALU.subtract, ALU.min).then_inc(s["hq_ready"], 1)
                    link(nc.vector.tensor_scalar(fs[p][:, 0:1], g4[p][:, 0:1], gam[:, 0:1], 1.0 / 127.0, ALU.mult, ALU.mult))
                    link(nc.vector.tensor_scalar(fs[p][:, 1:2], g4[p][:, 0:1], gam[:, 1:2], 1.0 / 127.0, ALU.mult, ALU.mult))
                    for f in range(FB):
                        fsl = slice(f * 512, (f + 1) * 512)
                        v.wait_ge(s["gate_done"], t * FB + f + 1)
                        nc.vector.scalar_tensor_tensor(out=zg[:, fsl], in0=bank[f % 2][:, :], scalar=fs[p][:, 0:1], in1=gb[:, fsl],
                                                       op0=ALU.mult, op1=ALU.add).then_inc(s["zg_ready"], 1)
                        v.wait_ge(s["val_done"], t * FB + f + 1)
                        nc.vector.scalar_tensor_tensor(out=zv[:, fsl], in0=bank[2 + f % 2][:, :], scalar=fs[p][:, 1:2], in1=vb[:, fsl],
                                                       op0=ALU.mult, op1=ALU.add).then_inc(s["zv_ready"], 1)
                    v.wait_ge(s["zv_ready"], t * FB + FB)
                    v.wait_ge(s["silu_ready"], t * FB + FB)
                    link(nc.vector.tensor_tensor(zv[:, :], zv[:, :], zg[:, :], ALU.mult))
                    link(nc.vector.tensor_reduce(a4[:, 0:1], zv[:, :], AXX, ALU.max, apply_absolute_value=True))
                    link(nc.vector.tensor_scalar(a4[:, 0:1], a4[:, 0:1], 1e-5, None, ALU.max))
                    link(nc.vector.reciprocal(a4[:, 1:2], a4[:, 0:1]))
                    link(nc.vector.tensor_scalar(a4[:, 2:3], a4[:, 1:2], 127.0, None, ALU.mult))
                    link(nc.vector.tensor_scalar(zg[:, :], zv[:, :], a4[:, 2:3], ROUND, ALU.mult, ALU.add))
                    v.wait_ge(s["aqT_done"], 2 * t)
                    nc.vector.tensor_scalar(aq[:, :], zg[:, :], ROUND, 127.0, ALU.subtract, ALU.min).then_inc(s["aq_ready"], 1)
                    link(nc.vector.tensor_scalar(fo[:, :], a4[:, 0:1], gam[:, 2:3], 1.0 / 127.0, ALU.mult, ALU.mult))
                    if p == 0:
                        v.wait_ge(s["stored"], i * 32)
                    v.wait_ge(s["out_done"], t + 1)
                    nc.vector.scalar_tensor_tensor(out=outt[p][:, :], in0=bank[5][:, :], scalar=fo[:, 0:1], in1=ob[:, :],
                                                   op0=ALU.mult, op1=ALU.add).then_inc(s["fo_ready"], 1)
                    v.wait_ge(s["fo_ready"], t + 1)
                    nc.vector.tensor_tensor(outt[p][:, :], outt[p][:, :], xt, ALU.add).then_inc(s["out_ready"], 1)

            tile_pairs(v, pair)


def build(nc, io):
    with ExitStack() as ctx:
        keep = {
            "x": ctx.enter_context(nc.sbuf_tensor("x", [P, NT, D], F32)),
            "cst": ctx.enter_context(nc.sbuf_tensor("cst", [P, C_ALL], F32)),
            "bank": [ctx.enter_context(nc.psum_tensor(f"bank{i}", [P, 512], F32)) for i in range(8)],
        }
        with ExitStack() as attn:
            keep["hhi"] = attn.enter_context(nc.sbuf_tensor("hhi", [P, KC, B * T], F16))
            keep["hlo"] = attn.enter_context(nc.sbuf_tensor("hlo", [P, KC, B * T], F16))
            keep["sc"] = attn.enter_context(nc.sbuf_tensor("sc", [P, 5, NS, B], F32))
            keep["dec"] = attn.enter_context(nc.sbuf_tensor("dec", [P, NS, B], F32))
            stage_norm_and_scalars(nc, io, keep)
            stage_delta_rule(nc, io, keep)
        stage_sets(nc, io, keep)
        stage_ffn(nc, io, keep)


_INS = ["x", "ctx_2048", "itok_Sx4_0_63", "L0_attn_Wq", "L0_attn_Wk", "L0_attn_Wv", "L0_attn_conv_q", "L0_attn_conv_k",
        "L0_attn_conv_v", "L0_attn_Wb", "L0_attn_Wa", "L0_attn_A_log", "L0_attn_dt_bias", "L0_attn_Wg", "L0_attn_norm_weight",
        "L0_attn_Wo", "L0_xattn_desc_router", "L0_xattn_W_q", "L0_xattn_b_q", "L0_ffn_gate_w", "L0_ffn_gate_b", "L0_ffn_val_w",
        "L0_ffn_val_b", "L0_ffn_out_w", "L0_ffn_out_b"]


def kernel(**inputs):
    import numpy as _np
    import concourse.bacc as _bacc
    from concourse import mybir as _mybir
    from concourse.bass_utils import run_bass_kernel_spmd as _run

    nc = _bacc.Bacc("TRN2", target_bir_lowering=False, num_devices=1)
    arrays, io = {}, {}
    for name in _INS:
        a = _np.ascontiguousarray(inputs[name])
        arrays[f"in_{name}_dram"] = a
        io[name] = nc.dram_tensor(f"in_{name}_dram", a.shape, _mybir.dt.from_np(a.dtype), kind="ExternalInput").ap()
    arrays["shape_constants"] = shape_constants()
    io["cst"] = nc.dram_tensor("shape_constants", arrays["shape_constants"].shape, _mybir.dt.float32, kind="ExternalInput").ap()
    io["out"] = nc.dram_tensor("out_0_dram", (B, T, D), _mybir.dt.float32, kind="ExternalOutput").ap()
    build(nc, io)
    r = _run(nc, [arrays], core_ids=[0])
    return r.results[0]["out_0_dram"]
```

```python
from contextlib import ExitStack

import numpy as np

import concourse.bass as bass
from concourse import mybir

P = 128
F32 = mybir.dt.float32
F16 = mybir.dt.float16
BF16 = mybir.dt.bfloat16
I32 = mybir.dt.int32
U32 = mybir.dt.uint32
ALU = mybir.AluOpType
ACT = mybir.ActivationFunctionType
AXX = mybir.AxisListType.X
ds = bass.ds

B, T, D = 4, 512, 512
H, DK, DV = 16, 96, 192
KC = D // P
NT = B * T // P
CH = T // P
HB = P // 2
LV = 6
QKV = 2 * DK + DV
NS = H * CH
FF = 4 * D
NSET = 64
TOPK_IN = 4
NQ = 4
SH, SW = 64.0, 1024.0
SHW = SH * SW
LN_EPS, EPS = 1e-5, 1e-6
SO = 4.0
NORM = (2 * SHW / SO) ** 2
ROUND = 12582912.0
G_, BETA, NBETA, EG, NBEG = range(5)

C_U, C_GT, C_ID = 0, P, 2 * P
C_M = 3 * P
C_I64 = C_M + (LV + 1) * HB
C_IOTA = C_I64 + HB
C_ALL = C_IOTA + NSET


def shape_constants():
    c = np.zeros((P, C_ALL), np.float32)
    r = np.arange(P)[:, None]
    t = np.arange(P)[None, :]
    c[:, C_U:C_U + P] = r <= t
    c[:, C_GT:C_GT + P] = r > t
    c[:, C_ID:C_ID + P] = r == t
    h = np.arange(HB)[None, :]
    for lv in range(LV):
        s = 1 << lv
        c[:, C_M + lv * HB:C_M + (lv + 1) * HB] = ((r % HB) // s % 2 == 1) & (h // s == (r % HB) // s - 1)
    c[:, C_M + LV * HB:C_M + (LV + 1) * HB] = r >= HB
    c[:, C_I64:C_I64 + HB] = (r % HB) == h
    c[:, C_IOTA:C_IOTA + NSET] = np.arange(NSET)[None, :]
    return c


def over(ap, axis, n):
    a = ap.unsqueeze(axis)
    shape = list(a.shape)
    shape[axis] = n
    return a.broadcast_to(shape)


def tile_quads(eng, body):
    body(0)
    with eng.Fori(1, NT // 4) as i:
        body(i)


def stage_norm_and_scalars(nc, io, keep):
    x_sb, hhi, hlo, sc, dec, cst, bank = (keep[k] for k in ("x", "hhi", "hlo", "sc", "dec", "cst", "bank"))
    with ExitStack() as ctx:
        def sb(name, shape, dt=F32):
            return ctx.enter_context(nc.sbuf_tensor("n_" + name, shape, dt))

        def sem(name):
            return ctx.enter_context(nc.semaphore("n_" + name))

        stats = sb("stats", [P, 6])
        mv = sb("mv", [P, NT, 2])
        var = sb("var", [P, NT])
        half = sb("half", [P, NT])
        rstd = sb("rstd", [P, NT])
        hn = [sb(f"hn{p}", [P, D]) for p in range(4)]
        wab = sb("wab", [P, KC, 2 * H])
        wabh = sb("wabh", [P, KC, 2 * H], F16)
        wabl = sb("wabl", [P, KC, 2 * H], F16)
        dtb = sb("dtb", [P, H])
        alog = sb("alog", [P, H])
        z = sb("z", [P, NT, H])
        az = sb("az", [P, NT, H])
        ez = sb("ez", [P, NT, H])
        lz = sb("lz", [P, NT, H])
        rz = sb("rz", [P, NT, H])
        eb = sb("eb", [P, NT, H])
        bt = sb("bt", [P, NT, H])
        ones = sb("ones", [P, P])
        x_in = [sem(f"x_in{b}") for b in range(B)]
        par_in = sem("par_in")
        cst_in = sem("cst_in")
        stat = sem("stat")
        hn_ready = sem("hn_ready")
        hT_ready = sem("hT_ready")
        hi_ready = sem("hi_ready")
        lo_ready = sem("lo_ready")
        ab_ready = sem("ab_ready")
        v_small = sem("v_small")
        a_small = sem("a_small")
        g_small = sem("g_small")
        sum_ready = sem("sum_ready")
        quad = (bank[0], bank[1], bank[4], bank[5])
        block = ctx.enter_context(nc.Block())

        @block.sync
        def _(sp):
            for b in range(B):
                sp.dma_start(x_sb[:, b * CH:(b + 1) * CH, :], io["x"][b].rearrange("(c p) d -> p c d", p=P)).then_inc(x_in[b], 16)
                if b == 0:
                    sp.dma_start(cst[:, :], io["cst"]).then_inc(cst_in, 16)
            sp.dma_start(wab[:, :, 0:H], io["L0_attn_Wa"].rearrange("(k p) h -> p k h", p=P)).then_inc(par_in, 16)
            sp.dma_start(wab[:, :, H:], io["L0_attn_Wb"].rearrange("(k p) h -> p k h", p=P)).then_inc(par_in, 16)
            sp.dma_start(dtb[:, :], io["L0_attn_dt_bias"].partition_broadcast(P)).then_inc(par_in, 16)
            sp.dma_start(alog[:, :], io["L0_attn_A_log"].partition_broadcast(P)).then_inc(par_in, 16)

        @block.gpsimd
        def _(pool):
            nc.gpsimd.memset(ones[:, :], 1.0).then_inc(g_small, 1)
            nc.gpsimd.memset(half[:, :], -0.5).then_inc(g_small, 1)
            pool.wait_ge(stat, 2 * NT)
            nc.gpsimd.tensor_scalar(var[:, :], mv[:, :, 1], LN_EPS, None, ALU.add).then_inc(g_small, 1)
            pool.wait_ge(g_small, 3)
            nc.gpsimd.tensor_tensor(rstd[:, :], var[:, :], half[:, :], ALU.pow).then_inc(g_small, 1)
            pool.wait_ge(par_in, 64)
            nc.gpsimd.tensor_scalar(wab[:, :, :], wab[:, :, :], SW, None, ALU.mult).then_inc(g_small, 1)
            pool.wait_ge(g_small, 5)
            nc.gpsimd.tensor_copy(wabh[:, :, :], wab[:, :, :]).then_inc(g_small, 1)
            pool.wait_ge(g_small, 6)
            nc.gpsimd.tensor_tensor(wabl[:, :, :], wab[:, :, :], wabh[:, :, :], ALU.subtract).then_inc(g_small, 1)

        @block.vector
        def _(v):
            for t in range(NT):
                if t % CH == 0:
                    v.wait_ge(x_in[t // CH], 16)
                if t:
                    v.wait_ge(stat, 2 * t)
                nc.vector.bn_stats(stats[:, :], x_sb[:, t, :]).then_inc(stat, 1)
                v.wait_ge(stat, 2 * t + 1)
                nc.vector.bn_aggr(mv[:, t, :], stats[:, :]).then_inc(stat, 1)
            v.wait_ge(g_small, 4)
            v.wait_ge(stat, 2 * NT)
            def four(i):
                for p in range(4):
                    if not isinstance(i, int):
                        v.wait_ge(hT_ready, i * 4 + p - 3)
                    nc.vector.tensor_scalar(hn[p][:, :], x_sb[:, ds(i * 4 + p, 1), :].squeeze(1), mv[:, ds(i * 4 + p, 1), 0],
                                            rstd[:, ds(i * 4 + p, 1)], ALU.subtract, ALU.mult).then_inc(hn_ready, 1)
                for p in range(4):
                    v.wait_ge(hi_ready, i * 4 + p + 1)
                    hs = ds((i * 4 + p) * P, P)
                    nc.vector.scalar_tensor_tensor(out=hlo[:, :, hs], in0=quad[p][:, :].rearrange("p (k t) -> p k t", k=KC),
                                                   scalar=SH, in1=hhi[:, :, hs], op0=ALU.mult, op1=ALU.subtract).then_inc(lo_ready, 1)

            tile_quads(v, four)
            v.wait_ge(ab_ready, 1)
            v.wait_ge(par_in, 64)
            ab = bank[2][:, :].rearrange("p (t h) -> p t h", t=NT)
            nc.vector.scalar_tensor_tensor(out=z[:, :, :], in0=ab[:, :, 0:H], scalar=1.0 / SHW, in1=over(dtb[:, :], 1, NT),
                                           op0=ALU.mult, op1=ALU.add).then_inc(v_small, 1)
            v.wait_ge(v_small, 1)
            nc.vector.tensor_scalar(az[:, :, :], z[:, :, :], -1.0, None, ALU.mult).then_inc(v_small, 1)
            v.wait_ge(v_small, 2)
            nc.vector.tensor_tensor(az[:, :, :], az[:, :, :], z[:, :, :], ALU.min).then_inc(v_small, 1)
            nc.vector.tensor_scalar(rz[:, :, :], z[:, :, :], 0.0, None, ALU.max).then_inc(v_small, 1)
            v.wait_ge(a_small, 4)
            v.wait_ge(v_small, 4)
            nc.vector.tensor_tensor(rz[:, :, :], rz[:, :, :], lz[:, :, :], ALU.add).then_inc(v_small, 1)
            v.wait_ge(v_small, 5)
            g_view = sc[:, G_, :, :].rearrange("p (h c) b -> p b c h", c=CH)
            for b in range(B):
                nc.vector.scalar_tensor_tensor(out=g_view[:, b], in0=rz[:, b * CH:(b + 1) * CH, :], scalar=-1.0,
                                               in1=over(alog[:, :], 1, CH), op0=ALU.mult, op1=ALU.mult).then_inc(v_small, 1)
            nc.vector.tensor_scalar(eb[:, :, :], eb[:, :, :], 1.0, None, ALU.add).then_inc(v_small, 1)
            v.wait_ge(v_small, 10)
            nc.vector.reciprocal(bt[:, :, :], eb[:, :, :]).then_inc(v_small, 1)
            v.wait_ge(v_small, 11)
            for kind, factor in ((BETA, 2.0), (NBETA, -2.0)):
                view = sc[:, kind, :, :].rearrange("p (h c) b -> p b c h", c=CH)
                for b in range(B):
                    nc.vector.tensor_scalar(view[:, b], bt[:, b * CH:(b + 1) * CH, :], factor, None, ALU.mult).then_inc(v_small, 1)
            v.wait_ge(a_small, 5)
            v.wait_ge(v_small, 19)
            nc.vector.tensor_tensor(sc[:, NBEG, :, :], sc[:, NBETA, :, :], sc[:, EG, :, :], ALU.mult).then_inc(v_small, 1)

        @block.scalar
        def _(a):
            def four(i):
                for p in range(4):
                    a.wait_ge(hT_ready, i * 4 + p + 1)
                    nc.scalar.activation(hhi[:, :, ds((i * 4 + p) * P, P)], quad[p][:, :].rearrange("p (k t) -> p k t", k=KC),
                                         ACT.Copy, scale=SH).then_inc(hi_ready, 1)

            tile_quads(a, four)
            a.wait_ge(par_in, 64)
            a.wait_ge(v_small, 4)
            nc.scalar.activation(ez[:, :, :], az[:, :, :], ACT.Exp).then_inc(a_small, 1)
            a.wait_ge(a_small, 1)
            nc.scalar.activation(lz[:, :, :], ez[:, :, :], ACT.Ln, bias=1.0).then_inc(a_small, 1)
            nc.scalar.activation(alog[:, :], alog[:, :], ACT.Exp).then_inc(a_small, 1)
            nc.scalar.activation(eb[:, :, :], bank[2][:, :].rearrange("p (t h) -> p t h", t=NT)[:, :, H:], ACT.Exp,
                                 scale=-1.0 / SHW).then_inc(a_small, 1)
            a.wait_ge(sum_ready, 1)
            nc.scalar.activation(sc[:, EG, :, :].rearrange("p n b -> p (n b)"), bank[3][:, 0:NS * B], ACT.Exp).then_inc(a_small, 1)
            nc.scalar.activation(dec[:, :, :].rearrange("p n b -> p (n b)"), bank[3][:, NS * B:], ACT.Exp).then_inc(a_small, 1)

        @block.tensor
        def _(pe):
            pe.wait_ge(cst_in, 16)
            def four(i):
                for p in range(4):
                    pe.wait_ge(hn_ready, i * 4 + p + 1)
                    if not isinstance(i, int):
                        pe.wait_ge(lo_ready, i * 4 + p - 3)
                    for k in range(KC):
                        last = nc.tensor.transpose(quad[p][:, k * P:(k + 1) * P], hn[p][:, k * P:(k + 1) * P], cst[:, C_ID:C_ID + P])
                    last.then_inc(hT_ready, 1)

            tile_quads(pe, four)
            pe.wait_ge(lo_ready, NT)
            pe.wait_ge(g_small, 7)
            for t in range(NT):
                terms = [(x, w, k) for x, w in ((hhi, wabh), (hhi, wabl), (hlo, wabh)) for k in range(KC)]
                for n, (x, w, k) in enumerate(terms):
                    last = nc.tensor.matmul(bank[2][:, t * 2 * H:(t + 1) * 2 * H], x[:, k, t * P:(t + 1) * P], w[:, k, :],
                                            start=(n == 0), stop=(n == len(terms) - 1))
            last.then_inc(ab_ready, 1)
            pe.wait_ge(v_small, 9)
            pe.wait_ge(g_small, 1)
            g_all = sc[:, G_, :, :].rearrange("p n b -> p (n b)")
            nc.tensor.matmul(bank[3][:, 0:NS * B], cst[:, C_U:C_U + P], g_all, start=True, stop=True)
            nc.tensor.matmul(bank[3][:, NS * B:], ones[:, :], g_all, start=True, stop=True).then_inc(sum_ready, 1)


class Step:

    def __init__(self, n, k, u, project=True, turn=True, recur=True, output=True):
        self.n, self.k, self.c = n, k, u % CH
        self.cp = (u + 2) % CH
        self.kp = k + 1 if self.c >= CH - 2 else k
        self.p, self.pm = u % 2, (u + 1) % 2
        self.wp = ((u + 2) // CH) % 2
        self.ws = self.wk = (u // CH) % 2
        self.wn = ((u - 1) // CH) % 2
        self.project, self.turn, self.recur, self.output = project, turn, recur, output


def all_steps(eng, body):
    body(Step(-2, -1, -2, turn=False, recur=False, output=False))
    body(Step(-1, -1, -1, recur=False, output=False))
    for u in range(2 * CH):
        body(Step(u, u // CH, u, output=u > 0))
    with eng.Fori(1, H // 2 - 1) as j:
        for u in range(2 * CH):
            body(Step(j * (2 * CH) + u, j * 2 + u // CH, u))
    for u in range(2 * CH):
        n = NS - 2 * CH + u
        body(Step(n, n // CH, u, project=n + 2 < NS, turn=n + 1 < NS))
    body(Step(NS, H, 0, project=False, turn=False, recur=False))


def stage_delta_rule(nc, io, keep):
    x_sb, hhi, hlo, sc, dec, cst, bank = (keep[k] for k in ("x", "hhi", "hlo", "sc", "dec", "cst", "bank"))
    with ExitStack() as ctx:
        def sb(name, shape, dt=F32):
            return ctx.enter_context(nc.sbuf_tensor("d_" + name, shape, dt))

        def sem(name):
            return ctx.enter_context(nc.semaphore("d_" + name))

        st = sb("st", [P, KC * DV + 2 * D])
        st_a = st[:, 0:KC * QKV].rearrange("p (k n) -> p k n", k=KC)
        st_g = st[:, 0:KC * DV].rearrange("p (k n) -> p k n", k=KC)
        st_o = st[:, KC * DV:].rearrange("p (i n) -> p i n", i=2)
        wa = [[sb(f"wa{q}{s}", [P, KC, QKV], F16) for s in "hl"] for q in range(2)]
        wg = [sb(f"wg{s}", [P, KC, DV], F16) for s in "hl"]
        wo = [[sb(f"wo{q}{s}", [P, 2, D], F16) for s in "hl"] for q in range(2)]
        nw = sb("nw", [P, 2])
        cw = sb("cw", [P, H, 3, 4])
        y = [sb(f"y{q}", [P, B, P]) for q in range(2)]
        th = sb("th", [P, B, P])
        qT = [sb(f"qT{q}", [P, B, P]) for q in range(CH)]
        yv = [sb(f"yv{q}", [P, 2, B, P]) for q in range(2)]
        tail = [sb(f"tail{q}", [P, 3, B, 3]) for q in range(2)]
        tok = sb("tok", [P, B, QKV])
        sq = sb("sq", [P, B, 2, DK])
        ss = sb("ss", [P, B, 2])
        sse = sb("sse", [P, B, 2])
        kap = sb("kap", [P, B, 2])
        mhalf = sb("mhalf", [P, B, 2])
        epsq = [sb(f"epsq{q}", [P, B]) for q in range(2)]
        V = [sb(f"V{q}", [P, B, DV]) for q in range(2)]
        K = [sb(f"K{q}", [P, B, DK]) for q in range(2)]
        kT = [sb(f"kT{q}", [DK, B, P]) for q in range(2)]
        Gm = sb("Gm", [P, B, P])
        E = sb("E", [P, B, P])
        Em = sb("Em", [P, B, P])
        LT = sb("LT", [P, B, P])
        PT = sb("PT", [P, B, P])
        nbM = sb("nbM", [P, LV + 1, B, HB])
        Y = sb("Y", [P, B * HB])
        X = sb("X", [P, 2 * B * HB])
        XT = sb("XT", [P, B, P])
        i8 = sb("i8", [P, 2 * B, HB], BF16)
        idb = sb("idb", [P, P], BF16)
        S = sb("S", [DK, B, DV])
        W = sb("W", [P, B, DV])
        Q = sb("Q", [P, B, DV])
        Dl = sb("Dl", [P, B, DV])
        K2 = sb("K2", [P, B, DK])
        thg = sb("thg", [P, 2 * DV])
        gate = sb("gate", [P, B, DV])
        O = sb("O", [P, B, DV])
        on = sb("on", [P, B, DV])
        junk = sb("junk", [P, B, DV])
        sso = sb("sso", [P, B])
        ms = sb("ms", [P, B])
        rn = sb("rn", [P, B])
        ohl = sb("ohl", [P, B, 3, P], F16)
        onT = sb("onT", [P, 3, B, P], F16)
        idh = sb("idh", [P, P], F16)

        names = """par_in st_a_in st_g_in st_o_in wa_scaled wg_scaled
            const_ready cw_ready wa_ready wg_ready wo_ready
            proj_done tap0_done conv_done tanh_done silu_done tok_done tok_read sq_done ss_done kappa_done V_ready K_ready
            kT_done kT_ready
            Gm_ready nbM_ready dif_done E_ready Em_ready gram_done qk_done LT_ready PT_ready
            ks_done qs_done W_ready qs_read yps_done Y_ready xps_done X_ready x21_done XT_ready
            gate_done gtanh_done gate_ready d_done D_ready pd_done O_ready K2_ready su_done S_ready
            ssq_done r_ready on_ready high_ready low_ready wo_scaled onT_done onT_ready wo_done x_added""".split()
        s = {name: sem(name) for name in names}
        block = ctx.enter_context(nc.Block())
        ident = cst[:, C_ID:C_ID + P]
        U = cst[:, C_U:C_U + P]

        held = keep["held"]

        def hold(eng, sem, value):
            eng.wait_ge(sem, value)
            if not isinstance(value, int):
                eng.sem_inc(held[str(eng.engine)], 1)

        def past(eng, name, value):
            if not isinstance(value, int):
                if eng.engine == nc.vector.engine:
                    eng.wait_ge(s[name], value)
                else:
                    hold(eng, s[name], value)
            elif value > 0:
                eng.wait_ge(s[name], value)

        @block.sync
        def _(sp):
            def load_a(h):
                if not isinstance(h, int) or h > 0:
                    hold(sp, s["wa_ready"], h)
                if not isinstance(h, int):
                    hold(sp, s["wg_ready"], h - 1)
                    hold(sp, s["wo_ready"], h - 1)
                for name, at, w in (("Wq", 0, DK), ("Wv", DK, DV), ("Wk", DK + DV, DK)):
                    src = io["L0_attn_" + name].rearrange("(k p) n -> p k n", p=P)
                    sp.dma_start(st_a[:, :, at:at + w], src[:, :, ds(h * w, w)]).then_inc(s["st_a_in"], 16)

            nwt = io["L0_attn_norm_weight"].rearrange("(p one) -> p one", one=1)
            sp.dma_start(nw[:, 0:1], nwt[0:P]).then_inc(s["par_in"], 16)
            for h in range(2):
                sp.dma_start(nw[h * HB:(h + 1) * HB, 1:2], nwt[P:DV]).then_inc(s["par_in"], 16)
            cq, ck, cv = (io["L0_attn_conv_" + n].rearrange("(h c) k -> c h k", h=H) for n in "qkv")
            v0, v1 = P - DK, 2 * P - DK
            sp.dma_start(cw[0:DK, :, 0, :], cq).then_inc(s["par_in"], 16)
            sp.dma_start(cw[DK:P, :, 0, :], cv[0:v0]).then_inc(s["par_in"], 16)
            sp.dma_start(cw[:, :, 1, :], cv[v0:v1]).then_inc(s["par_in"], 16)
            sp.dma_start(cw[0:P - DK, :, 2, :], cv[v1:DV]).then_inc(s["par_in"], 16)
            sp.dma_start(cw[P - DK:P, :, 2, :], ck).then_inc(s["par_in"], 16)
            load_a(0)
            load_a(1)

            def load_go(k):
                if isinstance(k, int):
                    hold(sp, s["wg_ready"], k)
                    hold(sp, s["wo_ready"], k)
                else:
                    hold(sp, s["wa_ready"], k + 2)
                sp.dma_start(st_g, io["L0_attn_Wg"].rearrange("(k p) n -> p k n", p=P)[:, :, ds(k * DV, DV)]).then_inc(s["st_g_in"], 16)
                sp.dma_start(st_o[:, 0, :], io["L0_attn_Wo"][ds(k * DV, P), :]).then_inc(s["st_o_in"], 16)
                for h in range(2):
                    sp.dma_start(st_o[h * HB:(h + 1) * HB, 1, :], io["L0_attn_Wo"][ds(k * DV + P, HB), :]).then_inc(s["st_o_in"], 16)

            with sp.Fori(0, H - 2) as k:
                load_go(k)
                load_a(k + 2)
            sp.wait_ge(s["wa_ready"], H)
            for k in range(H - 2, H):
                load_go(k)

        @block.gpsimd
        def _(pool):
            def prepare():
                nc.gpsimd.memset(mhalf[:, :, :], -0.5).then_inc(s["const_ready"], 1)
                nc.gpsimd.memset(XT[:, :, :], 0.0).then_inc(s["const_ready"], 1)
                nc.gpsimd.tensor_copy(i8[:, :, :], over(cst[:, C_I64:C_I64 + HB], 1, 2 * B)).then_inc(s["const_ready"], 1)
                nc.gpsimd.tensor_copy(idb[:, :], ident).then_inc(s["const_ready"], 1)
                nc.gpsimd.tensor_copy(idh[:, :], ident).then_inc(s["const_ready"], 1)
                hold(pool, s["par_in"], 16 * 8)
                nc.gpsimd.tensor_scalar(cw[:, :, :, :], cw[:, :, :, :], 0.5 / SHW, None, ALU.mult).then_inc(s["cw_ready"], 1)
                nc.gpsimd.tensor_scalar(nw[:, :], nw[:, :], SW, None, ALU.mult).then_inc(s["cw_ready"], 1)

            def split_a(h, q):
                hold(pool, s["st_a_in"], (h + 1) * 48)
                if not isinstance(h, int) or h >= 2:
                    hold(pool, s["proj_done"], (h - 1) * 3 * CH)
                scaled = s["wa_scaled"]
                nc.gpsimd.tensor_scalar(st_a[:, :, :], st_a[:, :, :], SW, None, ALU.mult).then_inc(scaled, 1)
                hold(pool, scaled, h * 2 + 1)
                nc.gpsimd.tensor_copy(wa[q][0][:, :, :], st_a[:, :, :]).then_inc(scaled, 1)
                hold(pool, scaled, h * 2 + 2)
                nc.gpsimd.tensor_tensor(wa[q][1][:, :, :], st_a[:, :, :], wa[q][0][:, :, :], ALU.subtract).then_inc(s["wa_ready"], 1)

            def split_g(k):
                hold(pool, s["st_g_in"], k * 16 + 16)
                hold(pool, s["gate_done"], 2 * CH * k)
                nc.gpsimd.tensor_scalar(st_g[:, :, :], st_g[:, :, :], SW, None, ALU.mult).then_inc(s["wg_scaled"], 1)
                hold(pool, s["wg_scaled"], k * 2 + 1)
                nc.gpsimd.tensor_copy(wg[0][:, :, :], st_g[:, :, :]).then_inc(s["wg_scaled"], 1)
                hold(pool, s["wg_scaled"], k * 2 + 2)
                nc.gpsimd.tensor_tensor(wg[1][:, :, :], st_g[:, :, :], wg[0][:, :, :], ALU.subtract).then_inc(s["wg_ready"], 1)

            def split_o(k, q):
                hold(pool, s["st_o_in"], k * 48 + 48)
                past(pool, "wo_done", B * CH * (k - 1))
                for i in range(2):
                    nc.gpsimd.tensor_scalar(st_o[:, i, :], st_o[:, i, :], nw[:, i:i + 1], None, ALU.mult).then_inc(s["wo_scaled"], 1)
                hold(pool, s["wo_scaled"], k * 3 + 2)
                nc.gpsimd.tensor_copy(wo[q][0][:, :, :], st_o[:, :, :]).then_inc(s["wo_scaled"], 1)
                hold(pool, s["wo_scaled"], k * 3 + 3)
                nc.gpsimd.tensor_tensor(wo[q][1][:, :, :], st_o[:, :, :], wo[q][0][:, :, :], ALU.subtract).then_inc(s["wo_ready"], 1)

            def exponents(n):
                past(pool, "dif_done", n)
                nc.gpsimd.tensor_tensor(Gm[:, :, :], over(U, 1, B),
                                        over(sc[:, G_, ds(n, 1), :].squeeze(1), 2, P), ALU.mult).then_inc(s["Gm_ready"], 1)

            def level_blocks(n):
                past(pool, "XT_ready", n)
                for l in range(LV + 1):
                    last = nc.gpsimd.tensor_tensor(nbM[:, l, :, :], over(cst[:, C_M + l * HB:C_M + (l + 1) * HB], 1, B),
                                                   over(sc[:, NBETA, ds(n, 1), :].squeeze(1), 2, HB), ALU.mult)
                last.then_inc(s["nbM_ready"], 1)

            def step(st):
                n, m, c = st.n, st.n + 1, st.c
                if st.output:
                    past(pool, "ssq_done", B * n)
                    nc.gpsimd.tensor_scalar(ms[:, :], sso[:, :], NORM / DV, None, ALU.mult).then_inc(s["r_ready"], 1)
                    past(pool, "r_ready", 3 * n - 2)
                    nc.gpsimd.tensor_tensor(ms[:, :], ms[:, :], epsq[st.pm][:, :], ALU.add).then_inc(s["r_ready"], 1)
                    past(pool, "r_ready", 3 * n - 1)
                    past(pool, "on_ready", B * n - B)
                    nc.gpsimd.tensor_tensor(rn[:, :], ms[:, :], mhalf[:, 0:2, :].rearrange("p a b -> p (a b)"), ALU.pow).then_inc(s["r_ready"], 1)
                if st.recur:
                    past(pool, "E_ready", n + 1)
                    past(pool, "PT_ready", n)
                    nc.gpsimd.tensor_tensor(Em[:, :, :], E[:, :, :], over(U, 1, B), ALU.mult).then_inc(s["Em_ready"], 1)
                    past(pool, "su_done", 2 * n)
                    for i in range(B):
                        nc.gpsimd.tensor_scalar(K2[:, i, :], K[st.p][:, i, :], E[:, i, P - 1:P], None, ALU.mult).then_inc(s["K2_ready"], 1)
                if st.turn:
                    past(pool, "tok_read", B * m + B)
                    past(pool, "ss_done", m)
                    for i, at in ((0, 0), (1, DK + DV)):
                        last = nc.gpsimd.tensor_tensor(sq[:, :, i, :], tok[:, :, at:at + DK], tok[:, :, at:at + DK], ALU.mult)
                    last.then_inc(s["sq_done"], 1)
                    past(pool, "W_ready", B * n)
                    nc.gpsimd.tensor_tensor(V[st.pm][:, :, :], tok[:, :, DK:DK + DV],
                                            over(sc[:, BETA, ds(m, 1), :].squeeze(1), 2, DV), ALU.mult).then_inc(s["V_ready"], 1)
                    past(pool, "ss_done", m + 1)
                    nc.gpsimd.tensor_scalar(sse[:, :, :], ss[:, :, :], EPS, None, ALU.add).then_inc(s["kappa_done"], 1)
                    past(pool, "kappa_done", 3 * m + 1)
                    nc.gpsimd.tensor_tensor(kap[:, :, :], sse[:, :, :], mhalf[:, :, :], ALU.pow).then_inc(s["kappa_done"], 1)
                    nc.gpsimd.tensor_scalar(epsq[st.pm][:, :], sse[:, :, 0], EPS * DK * NORM, None, ALU.mult).then_inc(s["kappa_done"], 1)
                    past(pool, "kappa_done", 3 * m + 3)
                    nc.gpsimd.tensor_tensor(K[st.pm][:, :, :], tok[:, :, DK + DV:], over(kap[:, :, 1], 2, DK),
                                            ALU.mult).then_inc(s["K_ready"], 1)
                    exponents(m)
                if st.recur and c == 0:
                    split_g(st.k)
                    split_o(st.k, st.wk)
                if c == CH - 1 and (st.recur or st.turn) and not (isinstance(n, int) and st.k + 2 >= H):
                    split_a(st.k + 2, st.ws)
                if st.turn:
                    level_blocks(m)

            prepare()
            hold(pool, s["const_ready"], 5)
            hold(pool, s["cw_ready"], 2)
            split_a(0, 0)
            all_steps(pool, step)

        @block.tensor
        def _(pe):
            pe.wait_ge(s["const_ready"], 5)

            def projection(st, t, part, parts):
                m = st.n + 2
                acc = bank[(st.p + t) % 2]
                if t == 0 and st.cp == 0 and part == 0:
                    past(pe, "wa_ready", st.kp + 1)
                if part == 0:
                    past(pe, "conv_done", 7 * (3 * m + t - 1))
                terms = [(w, x, k) for w, x in ((0, hhi), (1, hhi), (0, hlo)) for k in range(KC)]
                each = len(terms) // parts
                for e in range(part * each, (part + 1) * each):
                    w, x, k = terms[e]
                    last = nc.tensor.matmul(acc[:, :], wa[st.wp][w][:, k, t * P:(t + 1) * P],
                                            x[:, k, :].rearrange("p (b t) -> p b t", b=B)[:, :, st.cp * P:(st.cp + 1) * P],
                                            start=(e == 0), stop=(e == len(terms) - 1))
                if part == parts - 1:
                    last.then_inc(s["proj_done"], 1)

            def to_tokens(st, i):
                m = st.n + 1
                if i == 0:
                    past(pe, "silu_done", 3 * m + 3)
                    past(pe, "kT_ready", m)
                past(pe, "tok_read", B * m + i)
                for t in range(3):
                    src = qT[(st.c + 1) % CH][:, i, :] if t == 0 else yv[st.pm][:, t - 1, i, :]
                    last = nc.tensor.transpose(bank[2][:, t * P:(t + 1) * P], src, ident)
                last.then_inc(s["tok_done"], 1)

            def keys_back(st):
                m = st.n + 1
                pe.wait_ge(s["K_ready"], m + 1)
                pe.wait_ge(s["tok_read"], B * m + B)
                for i in range(B):
                    last = nc.tensor.transpose(bank[2][0:DK, i * P:(i + 1) * P], K[st.pm][:, i, :], ident)
                last.then_inc(s["kT_done"], 1)

            def levels(st, fill, run):
                n = st.n
                yb, xb = bank[3], bank[4]
                half = (slice(0, HB), slice(HB, P))
                i64 = cst[:, C_I64:C_I64 + HB]
                for l in range(LV):
                    if l == 0:
                        hold(pe, s["LT_ready"], n + 1)
                        hold(pe, s["XT_ready"], n)
                    else:
                        hold(pe, s["X_ready"], 8 * n + l)
                    for i in range(B):
                        for hf in half:
                            rhs = i64[hf, :] if l == 0 else X[hf, i * HB:(i + 1) * HB]
                            last = nc.tensor.matmul(yb[hf, i * HB:(i + 1) * HB], LT[hf, i, hf], rhs, start=True, stop=True)
                    last.then_inc(s["yps_done"], 1)
                    run(*next(fill))
                    hold(pe, s["Y_ready"], 7 * n + l + 1)
                    if l == 0:
                        hold(pe, s["X_ready"], 8 * n)
                        nc.tensor.matmul(xb[:, :], idb[:, :], i8[:, :, :].rearrange("p a b -> p (a b)"), start=True, stop=False,
                                         skip_group_check=True)
                        nc.tensor.matmul(xb[:, 0:B * HB], ident, Y[:, :], start=False, stop=False, skip_group_check=True)
                    for i in range(B):
                        for q, hf in enumerate(half):
                            mine = slice(i * HB, (i + 1) * HB)
                            turned = slice((B + i) * HB, (B + i + 1) * HB)
                            if l and (l < LV - 1 or q == 0):
                                nc.tensor.matmul(xb[hf, mine], X[hf, turned], Y[hf, mine], start=False, stop=(l == LV - 1),
                                                 skip_group_check=True)
                            rhs = i64[hf, :] if l == 0 else X[hf, turned]
                            last = nc.tensor.matmul(xb[hf, turned], Y[hf, mine], rhs, start=False, stop=(l == LV - 1),
                                                    skip_group_check=True)
                    last.then_inc(s["xps_done"], 1)
                    run(*next(fill))
                hold(pe, s["X_ready"], 8 * n + 8)
                for i in range(B):
                    last = nc.tensor.matmul(yb[HB:P, i * HB:(i + 1) * HB], LT[0:HB, i, HB:P], X[0:HB, i * HB:(i + 1) * HB],
                                            start=True, stop=True)
                last.then_inc(s["yps_done"], 1)
                run(*next(fill))
                hold(pe, s["Y_ready"], 7 * n + 7)
                for i in range(B):
                    last = nc.tensor.matmul(yb[0:HB, (B + i) * HB:(B + i + 1) * HB], Y[HB:P, i * HB:(i + 1) * HB], XT[HB:P, i, HB:P],
                                            start=True, stop=True)
                last.then_inc(s["x21_done"], 1)

            def gates(st, pair):
                n = st.n
                if st.c == 0 and pair == 0:
                    pe.wait_ge(s["wg_ready"], st.k + 1)
                if pair == 0:
                    past(pe, "W_ready", B * n + 4)
                    past(pe, "x_added", B * n - 2)
                else:
                    past(pe, "gate_ready", 2 * n + 1)
                for i in range(2):
                    tile = (2 * pair + i) * CH + st.c
                    terms = [(x, w, k) for x, w in ((hhi, 0), (hhi, 1), (hlo, 0)) for k in range(KC)]
                    for e, (x, w, k) in enumerate(terms):
                        last = nc.tensor.matmul(bank[6][:, i * DV:(i + 1) * DV], x[:, k, tile * P:(tile + 1) * P], wg[w][:, k, :],
                                                start=(e == 0), stop=(e == len(terms) - 1))
                last.then_inc(s["gate_done"], 1)

            def per_pair(st, done, at, waits, lhsT, rhs, rows=P, product=True):
                for pair in range(2):
                    for name, value in waits[pair]:
                        past(pe, name, value)
                    if not product:
                        pe.sem_inc(s[done], 1)
                        continue
                    for i in range(2):
                        e = 2 * pair + i
                        last = nc.tensor.matmul(bank[at[pair]][0:rows, i * DV:(i + 1) * DV], lhsT(e), rhs(e), start=True, stop=True)
                    last.then_inc(s[done], 1)

            def turn_output(st, part):
                n = st.n
                past(pe, "low_ready", n)
                if st.recur:
                    past(pe, *(("W_ready", B * n + 4), ("qs_read", B * n + 2))[part])
                for e, g in enumerate(((0, 1), (2,))[part]):
                    for i in range(B):
                        last = nc.tensor.transpose(bank[6 + part][:, :].bitcast(F16)[:, (e * B + i) * P:(e * B + i + 1) * P],
                                                   ohl[:, i, g, :], idh[:, :])
                last.then_inc(s["onT_done"], 1)

            def output(st, i):
                n = st.n
                if i == 0:
                    past(pe, "onT_ready", 2 * n)
                    past(pe, "wo_ready", st.k + 1 if st.c else st.k)
                    if st.recur:
                        past(pe, "qs_read", B * n + 4)
                if i == 3:
                    past(pe, "x_added", B * n - 3)
                wh, wl = wo[st.wn]
                terms = [(onT[:, 0, i, :], wh[:, 0, :]), (onT[:, 0, i, :], wl[:, 0, :]), (onT[:, 2, i, :], wh[:, 0, :]),
                         (onT[:, 1, i, :], wh[:, 1, :]), (onT[0:HB, 1, i, :], wl[0:HB, 1, :])]
                for e, (o, w) in enumerate(terms):
                    last = nc.tensor.matmul(bank[(5, 6, 7, 5)[i]][:, :], o, w, start=(e == 0), stop=(e == len(terms) - 1))
                last.then_inc(s["wo_done"], 1)

            def step(st):
                n, c = st.n, st.c
                turn = [lambda i=i: to_tokens(st, i) for i in range(B)] if st.turn else [None] * B
                back = [lambda: keys_back(st)] if st.turn else [None]
                proj = [[lambda t=t, e=e, q=q: projection(st, t, e, q) for e in range(q)] if st.project else [None] * q
                        for t, q in enumerate((3, 3, 4))]
                oT = [lambda h=h: turn_output(st, h) for h in range(2)] if st.output else [None] * 2
                wo_ = [lambda i=i: output(st, i) for i in range(B)] if st.output else [None] * B

                def run(*parts):
                    for part in parts:
                        if part is not None:
                            part()

                run(*proj[0])
                if not st.recur:
                    run(*turn, *proj[1], *proj[2], *oT, *wo_, *back)
                    return
                key, qry = kT[st.p], qT[c]
                past(pe, "Gm_ready", n + 1)
                past(pe, "O_ready", 2 * n)
                nc.tensor.matmul(bank[5][:, :], cst[:, C_GT:C_GT + P], Gm[:, :, :].rearrange("p b t -> p (b t)"),
                                 start=True, stop=True).then_inc(s["dif_done"], 1)
                run(turn[0])
                past(pe, "kT_ready", n + 1)
                past(pe, "S_ready", B * n + 2)
                for i in range(B):
                    last = nc.tensor.matmul(bank[6][:, i * P:(i + 1) * P], key[:, i, :], key[:, i, :], start=True, stop=True)
                last.then_inc(s["gram_done"], 1)
                past(pe, "S_ready", B * n + B)
                for i in range(B):
                    last = nc.tensor.matmul(bank[7][:, i * P:(i + 1) * P], key[:, i, :], qry[0:DK, i, :], start=True, stop=True)
                last.then_inc(s["qk_done"], 1)
                run(turn[1])
                per_pair(st, "ks_done", (5, 6), ([("E_ready", n + 1)], [("LT_ready", n + 1)]),
                         lambda i: key[:, i, :], lambda i: S[:, i, :], product=c > 0)
                run(turn[2])
                per_pair(st, "qs_done", (7, 5), ([("PT_ready", n + 1)], [("W_ready", B * n + 2)]),
                         lambda i: qry[0:DK, i, :], lambda i: S[:, i, :], product=c > 0)
                run(turn[3])
                levels(st, iter([[proj[1][0]], [proj[1][1]], [proj[1][2]], oT, [proj[2][0]], [wo_[0]], [proj[2][1]], [wo_[1]],
                                 [proj[2][2]], [wo_[2]], [proj[2][3]], [wo_[3]], back]), run)
                gates(st, 0)
                per_pair(st, "d_done", (7, 5), ([("XT_ready", n + 1), ("W_ready", B * n + 2), ("x_added", B * n - 1), ("qs_read", B * n + 2)],
                                                [("W_ready", B * n + 4), ("x_added", B * n), ("qs_read", B * n + 4)]),
                         lambda i: XT[:, i, :], lambda i: W[:, i, :])
                gates(st, 1)
                per_pair(st, "pd_done", (7, 5), ([("D_ready", 2 * n + 1)], [("D_ready", 2 * n + 2)]),
                         lambda i: PT[:, i, :], lambda i: Dl[:, i, :])
                per_pair(st, "su_done", (6, 7), ([("gate_ready", 2 * n + 2), ("K2_ready", B * n + B)], [("O_ready", 2 * n + 1)]),
                         lambda i: K2[:, i, :], lambda i: Dl[:, i, :], rows=DK, product=c < CH - 1)

            all_steps(pe, step)

        @block.scalar
        def _(a):
            def tap0(st, t):
                q = 3 * (st.n + 2) + t
                past(a, "silu_done", q - 1)
                past(a, "proj_done", q + 1)
                nc.scalar.activation(y[(st.p + t) % 2][:, :, :].rearrange("p b t -> p (b t)"), bank[(st.p + t) % 2][:, :], ACT.Copy,
                                     scale=cw[:, ds(st.kp, 1), t, 3]).then_inc(s["tap0_done"], 1)

            def tanh(st, t):
                q = 3 * (st.n + 2) + t
                past(a, "conv_done", 7 * q + 7)
                past(a, "silu_done", q)
                nc.scalar.activation(th[:, :, :], y[(st.p + t) % 2][:, :, :], ACT.Tanh).then_inc(s["tanh_done"], 1)

            def tokens(st, i):
                m = st.n + 1
                past(a, "tok_done", B * m + i + 1)
                if i == 0:
                    past(a, "K_ready", m)
                nc.scalar.activation(tok[:, i, :], bank[2][:, 0:QKV], ACT.Copy).then_inc(s["tok_read"], 1)

            def step(st):
                n = st.n

                def decay():
                    past(a, "dif_done", n + 1)
                    past(a, "LT_ready", n)
                    past(a, "K2_ready", B * n)
                    nc.scalar.activation(E[:, :, :].rearrange("p b t -> p (b t)"), bank[5][:, :], ACT.Exp).then_inc(s["E_ready"], 1)

                def copy_x(l):
                    past(a, "xps_done", LV * n + l + 1)
                    if l < LV - 1:
                        nc.scalar.activation(X[:, :], bank[4][:, :], ACT.Copy).then_inc(s["X_ready"], 1)
                        return
                    nc.scalar.activation(X[0:HB, 0:B * HB], bank[4][0:HB, 0:B * HB], ACT.Copy).then_inc(s["X_ready"], 1)
                    past(a, "d_done", 2 * n)
                    for hf in (slice(0, HB), slice(HB, P)):
                        nc.scalar.activation(XT[hf, :, hf], bank[4][hf, B * HB:].rearrange("p (b t) -> p b t", b=B),
                                             ACT.Copy).then_inc(s["X_ready"], 1)

                def read_qs(pair):
                    past(a, "O_ready", 2 * n)
                    past(a, "qs_done", 2 * n + pair + 1)
                    if st.c == 0:
                        a.sem_inc(s["qs_read"], 2)
                        return
                    for i in (2 * pair, 2 * pair + 1):
                        nc.scalar.activation(Q[:, i, :], bank[(7, 5)[pair]][:, (i % 2) * DV:(i % 2 + 1) * DV], ACT.Copy,
                                             scale=sc[:, EG, ds(n, 1), i]).then_inc(s["qs_read"], 1)

                def gate_tanh(pair):
                    past(a, "gate_done", 2 * n + pair + 1)
                    past(a, "gate_ready", 2 * n + pair)
                    nc.scalar.activation(thg[:, :], bank[6][:, 0:2 * DV], ACT.Tanh, scale=0.5 / SHW).then_inc(s["gtanh_done"], 1)

                def read_d(pair):
                    past(a, "d_done", 2 * n + pair + 1)
                    past(a, "su_done", 2 * n)
                    nc.scalar.activation(Dl[:, 2 * pair:2 * pair + 2, :].rearrange("p b v -> p (b v)"), bank[(7, 5)[pair]][:, 0:2 * DV],
                                         ACT.Copy).then_inc(s["D_ready"], 1)

                def squares():
                    past(a, "ssq_done", B * n)
                    past(a, "r_ready", 3 * n)
                    for i in range(B):
                        if i % 2 == 0:
                            past(a, "O_ready", 2 * n + i // 2 + 1)
                        nc.scalar.activation(junk[:, i, :], O[:, i, :], ACT.Square, accum_out=sso[:, i:i + 1]).then_inc(s["ssq_done"], 1)

                def high():
                    past(a, "on_ready", B * n)
                    past(a, "onT_done", 2 * n - 2)
                    nc.scalar.activation(ohl[:, :, :, :].rearrange("p b g t -> p b (g t)")[:, :, 0:DV], on[:, :, :],
                                         ACT.Copy).then_inc(s["high_ready"], 1)

                def read_onT(part):
                    past(a, "onT_done", 2 * n - 1 + part)
                    past(a, "wo_done", B * n - B)
                    w = (2, 1)[part]
                    nc.scalar.activation(onT[:, 2 * part:2 * part + w, :, :].rearrange("p g b t -> p (g b t)"),
                                         bank[6 + part][:, :].bitcast(F16)[:, 0:w * B * P], ACT.Copy).then_inc(s["onT_ready"], 1)

                def read_kT():
                    past(a, "kT_done", n + 2)
                    nc.scalar.activation(kT[st.pm][:, :, :].rearrange("p b t -> p (b t)"), bank[2][0:DK, :], ACT.Copy).then_inc(s["kT_ready"], 1)

                P_, T_, R_, O_ = st.project, st.turn, st.recur, st.output
                for go, what in ((P_, lambda: tap0(st, 0)), (R_, decay), (T_, lambda: tokens(st, 0)), (T_, lambda: tokens(st, 1)),
                                 (T_, lambda: tokens(st, 2)), (P_, lambda: tanh(st, 0)), (R_, lambda: read_qs(0)),
                                 (T_, lambda: tokens(st, 3)), (R_, lambda: read_qs(1)), (R_, lambda: copy_x(0)), (O_, high),
                                 (P_, lambda: tap0(st, 1)), (R_, lambda: copy_x(1)), (O_, lambda: read_onT(0)), (O_, lambda: read_onT(1)),
                                 (R_, lambda: copy_x(2)), (P_, lambda: tanh(st, 1)), (R_, lambda: copy_x(3)), (R_, lambda: copy_x(4)),
                                 (P_, lambda: tap0(st, 2)), (R_, lambda: copy_x(5)), (T_, read_kT), (R_, lambda: gate_tanh(0)),
                                 (R_, lambda: read_d(0)), (R_, lambda: read_d(1)), (P_, lambda: tanh(st, 2)), (R_, lambda: gate_tanh(1)),
                                 (R_, squares)):
                    if go:
                        what()

            a.wait_ge(s["cw_ready"], 2)
            all_steps(a, step)

        @block.vector
        def _(v):
            def conv(st, t, tap):
                q = 3 * (st.n + 2) + t
                if tap == 1:
                    v.wait_ge(s["tap0_done"], q + 1)
                else:
                    v.wait_ge(s["conv_done"], 7 * q + tap - 1)
                yy, pp = y[(st.p + t) % 2], bank[(st.p + t) % 2][:, :].rearrange("p (b t) -> p b t", b=B)
                nc.vector.scalar_tensor_tensor(out=yy[:, :, tap:], in0=pp[:, :, 0:P - tap], scalar=cw[:, ds(st.kp, 1), t, 3 - tap],
                                               in1=yy[:, :, tap:], op0=ALU.mult, op1=ALU.add).then_inc(s["conv_done"], 1)
                if tap < 3:
                    return
                if st.cp:
                    old = tail[st.pm][:, t, :, :]
                    for back in (1, 2, 3):
                        v.wait_ge(s["conv_done"], 7 * q + 2 + back)
                        nc.vector.scalar_tensor_tensor(out=yy[:, :, 0:back], in0=old[:, :, 3 - back:], scalar=cw[:, ds(st.kp, 1), t, 3 - back],
                                                       in1=yy[:, :, 0:back], op0=ALU.mult, op1=ALU.add).then_inc(s["conv_done"], 1)
                nc.vector.tensor_copy(tail[st.p][:, t, :, :], pp[:, :, P - 3:]).then_inc(s["conv_done"], 1 if st.cp else 4)

            def silu(st, t):
                q = 3 * (st.n + 2) + t
                v.wait_ge(s["tanh_done"], q + 1)
                v.wait_ge(s["conv_done"], 7 * q + 7)
                if t == 0:
                    past(v, "qs_done", 2 * st.n - 2)
                    dst = qT[st.cp][:, :, :]
                else:
                    past(v, "tok_done", B * (st.n + 1))
                    dst = yv[st.p][:, t - 1, :, :]
                nc.vector.scalar_tensor_tensor(out=dst, in0=th[:, :, :], scalar=1.0, in1=y[(st.p + t) % 2][:, :, :],
                                               op0=ALU.add, op1=ALU.mult).then_inc(s["silu_done"], 1)

            def step(st):
                n, m, c = st.n, st.n + 1, st.c

                def level(l):
                    rows = slice(0, P) if l < LV else slice(HB, P)
                    v.wait_ge(s["yps_done"], 7 * n + l + 1)
                    if l == 0:
                        v.wait_ge(s["nbM_ready"], n + 1)
                    nc.vector.tensor_tensor(Y[rows, :], bank[3][rows, 0:B * HB], nbM[rows, l, :, :].rearrange("p b t -> p (b t)"),
                                            ALU.mult).then_inc(s["Y_ready"], 1)

                def w_pair(pair):
                    v.wait_ge(s["ks_done"], 2 * n + pair + 1)
                    if pair == 0:
                        past(v, "d_done", 2 * n)
                        past(v, "V_ready", n + 1)
                    if c == 0:
                        two = slice(2 * pair, 2 * pair + 2)
                        nc.vector.tensor_copy(W[:, two, :], V[st.p][:, two, :]).then_inc(s["W_ready"], 2)
                        return
                    for i in (2 * pair, 2 * pair + 1):
                        nc.vector.scalar_tensor_tensor(out=W[:, i, :], in0=bank[5 + pair][:, (i % 2) * DV:(i % 2 + 1) * DV],
                                                       scalar=sc[:, NBEG, ds(n, 1), i], in1=V[st.p][:, i, :],
                                                       op0=ALU.mult, op1=ALU.add).then_inc(s["W_ready"], 1)

                def gate_pair(pair):
                    v.wait_ge(s["gtanh_done"], 2 * n + pair + 1)
                    nc.vector.scalar_tensor_tensor(out=gate[:, 2 * pair:2 * pair + 2, :].rearrange("p b v -> p (b v)"), in0=thg[:, :],
                                                   scalar=1.0, in1=bank[6][:, 0:2 * DV], op0=ALU.add, op1=ALU.mult).then_inc(s["gate_ready"], 1)

                def out_pair(pair):
                    v.wait_ge(s["pd_done"], 2 * n + pair + 1)
                    v.wait_ge(s["qs_read"], B * n + 2 * pair + 2)
                    past(v, "ssq_done", B * n)
                    two = slice(2 * pair, 2 * pair + 2)
                    if c == 0:
                        nc.vector.tensor_copy(O[:, two, :].rearrange("p b v -> p (b v)"), bank[(7, 5)[pair]][:, 0:2 * DV]).then_inc(s["O_ready"], 1)
                        return
                    nc.vector.tensor_tensor(O[:, two, :].rearrange("p b v -> p (b v)"), bank[(7, 5)[pair]][:, 0:2 * DV],
                                            Q[:, two, :].rearrange("p b v -> p (b v)"), ALU.add).then_inc(s["O_ready"], 1)

                def join():
                    v.wait_ge(s["x21_done"], n + 1)
                    nc.vector.tensor_copy(XT[0:HB, :, HB:P], bank[3][0:HB, B * HB:].rearrange("p (b t) -> p b t", b=B)).then_inc(s["XT_ready"], 1)

                def masked():
                    v.wait_ge(s["E_ready"], n + 1)
                    v.wait_ge(s["gram_done"], n + 1)
                    past(v, "yps_done", 7 * n)
                    nc.vector.tensor_tensor(LT[:, :, :].rearrange("p b t -> p (b t)"), bank[6][:, :],
                                            E[:, :, :].rearrange("p b t -> p (b t)"), ALU.mult).then_inc(s["LT_ready"], 1)
                    v.wait_ge(s["Em_ready"], n + 1)
                    v.wait_ge(s["qk_done"], n + 1)
                    past(v, "pd_done", 2 * n)
                    nc.vector.tensor_tensor(PT[:, :, :].rearrange("p b t -> p (b t)"), bank[7][:, :],
                                            Em[:, :, :].rearrange("p b t -> p (b t)"), ALU.mult).then_inc(s["PT_ready"], 1)

                def state():
                    for i in range(B):
                        if i % 2 == 0:
                            v.wait_ge(s["su_done"], 2 * n + i // 2 + 1)
                        if c < CH - 1:
                            nc.vector.scalar_tensor_tensor(out=S[:, i, :], in0=S[:, i, :], scalar=dec[0:DK, ds(n, 1), i],
                                                           in1=bank[6 + i // 2][0:DK, (i % 2) * DV:(i % 2 + 1) * DV],
                                                           op0=ALU.mult, op1=ALU.add).then_inc(s["S_ready"], 1)
                        elif i % 2 == 1:
                            nc.vector.memset(S[:, i - 1:i + 1, :], 0.0).then_inc(s["S_ready"], 2)

                def norms():
                    v.wait_ge(s["sq_done"], m + 1)
                    past(v, "kappa_done", 3 * m)
                    nc.vector.tensor_reduce(ss[:, :, :], sq[:, :, :, :], AXX, ALU.add).then_inc(s["ss_done"], 1)

                def gated():
                    v.wait_ge(s["r_ready"], 3 * n)
                    v.wait_ge(s["O_ready"], 2 * n)
                    v.wait_ge(s["gate_ready"], 2 * n)
                    past(v, "low_ready", n - 1)
                    for i in range(B):
                        nc.vector.scalar_tensor_tensor(out=on[:, i, :], in0=O[:, i, :], scalar=rn[:, i:i + 1], in1=gate[:, i, :],
                                                       op0=ALU.mult, op1=ALU.mult).then_inc(s["on_ready"], 1)

                def low():
                    v.wait_ge(s["high_ready"], n)
                    past(v, "onT_done", 2 * n - 2)
                    flat = ohl[:, :, :, :].rearrange("p b g t -> p b (g t)")
                    nc.vector.tensor_tensor(ohl[:, :, 2, :], on[:, :, 0:P], ohl[:, :, 0, :], ALU.subtract)
                    nc.vector.tensor_tensor(flat[:, :, DV:2 * P], on[:, :, P:DV], flat[:, :, P:DV], ALU.subtract).then_inc(s["low_ready"], 1)

                def add_x(i):
                    v.wait_ge(s["wo_done"], B * (n - 1) + i + 1)
                    xs = x_sb[:, i * CH + (c - 1) % CH, :]
                    nc.vector.scalar_tensor_tensor(out=xs, in0=bank[(5, 6, 7, 5)[i]][:, :], scalar=1.0 / (SO * SW), in1=xs,
                                                   op0=ALU.mult, op1=ALU.add).then_inc(s["x_added"], 1)

                P_, T_, R_, O_ = st.project, st.turn, st.recur, st.output
                for go, what in ((P_, lambda: conv(st, 0, 1)), (P_, lambda: conv(st, 0, 2)),
                                 (R_, masked), (P_, lambda: conv(st, 0, 3)), (R_, lambda: w_pair(0)), (R_, lambda: w_pair(1)), (P_, lambda: silu(st, 0)), (O_, gated),
                                 (R_, lambda: level(0)), (T_, norms), (R_, lambda: level(1)), (O_, low), (P_, lambda: conv(st, 1, 1)),
                                 (P_, lambda: conv(st, 1, 2)), (R_, lambda: level(2)), (P_, lambda: conv(st, 1, 3)), (R_, lambda: level(3)),
                                 (O_, lambda: add_x(0)), (P_, lambda: silu(st, 1)), (R_, lambda: level(4)), (O_, lambda: add_x(1)),
                                 (R_, lambda: level(5)), (P_, lambda: conv(st, 2, 1)), (P_, lambda: conv(st, 2, 2)), (R_, lambda: level(6)),
                                 (O_, lambda: add_x(2)), (R_, join), (O_, lambda: add_x(3)), (P_, lambda: conv(st, 2, 3)),
                                 (R_, lambda: gate_pair(0)), (P_, lambda: silu(st, 2)), (R_, lambda: gate_pair(1)),
                                 (R_, lambda: out_pair(0)), (R_, lambda: out_pair(1)), (R_, state)):
                    if go:
                        what()

            nc.vector.memset(S[:, :, :], 0.0).then_inc(s["S_ready"], B)
            v.wait_ge(s["cw_ready"], 2)
            all_steps(v, step)


def weight_quarter(io, w, q):
    if w < 2:
        return io[("L0_ffn_gate_w", "L0_ffn_val_w")[w]].rearrange("(k p) d -> p k d", p=P)[:, q * NQ:(q + 1) * NQ, :]
    return io["L0_ffn_out_w"].rearrange("(k p) (q d) -> p q k d", p=P, q=NQ)[:, q]


def overlapped_pairs(eng, first, second):
    first(0)
    first(1)
    second(0)
    with eng.Fori(1, NT // 2 - 1) as i:
        first(i + 1)
        second(i)
    second(NT // 2 - 1)


def stage_sets(nc, io, keep):
    x_sb, cst, bank, st, st_in, ffn_mv = (keep[k] for k in ("x", "cst", "bank", "st", "st_in", "ffn_mv"))
    with ExitStack() as ctx:
        def sb(name, shape, dt=F32):
            return ctx.enter_context(nc.sbuf_tensor("s_" + name, shape, dt))

        def sem(name):
            return ctx.enter_context(nc.semaphore("s_" + name))

        R = sb("R", [NSET, D])
        RT = sb("RT", [P, KC, NSET])
        Wq = sb("Wq", [P, KC, D])
        M = sb("M", [P, KC, NSET])
        bq = sb("bq", [P, KC])
        crow = sb("crow", [1, NSET])
        one = sb("one", [1, P])
        itok = sb("itok", [P, CH, TOPK_IN], I32)
        itf = sb("itf", [P, CH, TOPK_IN])
        bias = sb("bias", [P, CH, NSET])
        ctxs = sb("ctxs", [NSET, B, D])
        stats = sb("stats", [P, 6])
        mv = sb("mv", [P, NT, 2])
        var = sb("var", [P, NT])
        half = sb("half", [P, NT])
        rstd = sb("rstd", [P, NT])
        hn = [sb(f"hn{p}", [P, D]) for p in range(2)]
        hT = [sb(f"hT{p}", [P, KC, P]) for p in range(2)]
        score = sb("score", [P, NT, NSET])
        top = sb("top", [P, NT, 8])
        topi = sb("topi", [P, NT, 8], U32)
        idx = sb("idx", [P, NT, 2])
        gap = sb("gap", [P, NT])
        eg = sb("eg", [P, NT])
        den = sb("den", [P, NT])
        w0 = sb("w0", [P, NT])
        w1 = sb("w1", [P, NT])
        wt = sb("wt", [P, NT, NSET])
        wt1 = sb("wt1", [P, NT, NSET])
        wT = [sb(f"wT{p}", [NSET, P]) for p in range(2)]
        par_in = sem("par_in")
        small = sem("small")
        vs = sem("vs")
        vlink = sem("vlink")
        tops = sem("tops")
        stat = sem("stat")
        r_done = sem("r_done")
        rT_ready = sem("rT_ready")
        m_done = sem("m_done")
        M_ready = sem("M_ready")
        bias_ready = sem("bias_ready")
        hn_ready = [sem(f"hn_ready{p}") for p in range(2)]
        hT_done = [sem(f"hT_done{p}") for p in range(2)]
        hT_ready = [sem(f"hT_ready{p}") for p in range(2)]
        sc_done = [sem(f"sc_done{p}") for p in range(2)]
        score_ready = [sem(f"score_ready{p}") for p in range(2)]
        eg_ready = sem("eg_ready")
        wt_ready = sem("wt_ready")
        wT_done = [sem(f"wT_done{p}") for p in range(2)]
        wT_ready = [sem(f"wT_ready{p}") for p in range(2)]
        o_done = [sem(f"o_done{p}") for p in range(2)]
        added = [sem(f"added{p}") for p in range(2)]
        block = ctx.enter_context(nc.Block())
        ident = cst[:, C_ID:C_ID + P]
        iota = cst[:, C_IOTA:C_IOTA + NSET]

        @block.sync
        def _(sp):
            sp.dma_start(R[:, :], io["L0_xattn_desc_router"]).then_inc(par_in, 16)
            sp.dma_start(Wq[:, :, :], io["L0_xattn_W_q"].rearrange("(k p) d -> p k d", p=P)).then_inc(par_in, 16)
            sp.dma_start(bq[:, :], io["L0_xattn_b_q"].rearrange("(k p) -> p k", p=P), allow_slow_non_contiguous=True).then_inc(par_in, 16)
            sp.dma_start(itok[:, :, :], io["itok_Sx4_0_63"].rearrange("(c p) k -> p c k", p=P)).then_inc(par_in, 16)
            sp.dma_start(ctxs[:, :, :], io["ctx_2048"].rearrange("b n d -> n b d")).then_inc(par_in, 16)
            for q in range(NQ):
                sp.dma_start(st[q][:, :, :], weight_quarter(io, 0, q)).then_inc(st_in[q], 16)

        @block.gpsimd
        def _(pool):
            nc.gpsimd.memset(half[:, :], -0.5).then_inc(small, 1)
            nc.gpsimd.memset(one[:, :], 1.0).then_inc(small, 1)
            pool.wait_ge(stat, 2 * NT)
            nc.gpsimd.tensor_scalar(var[:, :], mv[:, :, 1], LN_EPS, None, ALU.add).then_inc(small, 1)
            pool.wait_ge(small, 3)
            nc.gpsimd.tensor_tensor(rstd[:, :], var[:, :], half[:, :], ALU.pow).then_inc(small, 1)

        @block.tensor
        def _(pe):
            pe.wait_ge(par_in, 80)
            for k in range(KC):
                last = nc.tensor.transpose(bank[0][:, k * NSET:(k + 1) * NSET], R[:, k * P:(k + 1) * P], ident[0:NSET, 0:NSET])
            last.then_inc(r_done, 1)
            pe.wait_ge(rT_ready, 1)
            for d in range(KC):
                for e in range(KC):
                    last = nc.tensor.matmul(bank[1][:, d * NSET:(d + 1) * NSET], Wq[:, e, d * P:(d + 1) * P], RT[:, e, :],
                                            start=(e == 0), stop=(e == KC - 1))
            for e in range(KC):
                last = nc.tensor.matmul(bank[1][0:1, KC * NSET:(KC + 1) * NSET], bq[:, e:e + 1], RT[:, e, :],
                                        start=(e == 0), stop=(e == KC - 1))
            last.then_inc(m_done, 1)
            pe.wait_ge(M_ready, 2)
            pe.wait_ge(small, 2)
            def turn(i):
                for p in range(2):
                    pe.wait_ge(hn_ready[p], i + 1)
                    if not isinstance(i, int) or i:
                        pe.wait_ge(hT_ready[p], i)
                    for k in range(KC):
                        last = nc.tensor.transpose(bank[2 + p][:, k * P:(k + 1) * P], hn[p][:, k * P:(k + 1) * P], ident)
                    last.then_inc(hT_done[p], 1)

            def scores(i):
                for p in range(2):
                    pe.wait_ge(hT_ready[p], i + 1)
                    if not isinstance(i, int) or i:
                        pe.wait_ge(score_ready[p], i)
                    for k in range(KC):
                        nc.tensor.matmul(bank[4 + p][:, 0:NSET], hT[p][:, k, :], M[:, k, :], start=(k == 0), stop=False)
                    nc.tensor.matmul(bank[4 + p][:, 0:NSET], one[0:1, :], crow[0:1, :], start=False, stop=True).then_inc(sc_done[p], 1)

            overlapped_pairs(pe, turn, scores)
            pe.wait_ge(wt_ready, 1)

            def turn_weights(t):
                p, i = t % 2, t // 2
                if i:
                    pe.wait_ge(wT_ready[p], i)
                nc.tensor.transpose(bank[6 + p][0:NSET, 0:P], wt[:, t, :], ident).then_inc(wT_done[p], 1)

            turn_weights(0)
            for t in range(NT):
                p, i = t % 2, t // 2
                if t + 1 < NT:
                    turn_weights(t + 1)
                pe.wait_ge(wT_ready[p], i + 1)
                if i:
                    pe.wait_ge(added[p], i)
                nc.tensor.matmul(bank[p][:, :], wT[p][:, :], ctxs[:, t // CH, :], start=True, stop=True).then_inc(o_done[p], 1)

        @block.scalar
        def _(a):
            a.wait_ge(r_done, 1)
            nc.scalar.activation(RT[:, :, :].rearrange("p k n -> p (k n)"), bank[0][:, 0:KC * NSET], ACT.Copy).then_inc(rT_ready, 1)
            a.wait_ge(m_done, 1)
            nc.scalar.activation(M[:, :, :].rearrange("p k n -> p (k n)"), bank[1][:, 0:KC * NSET], ACT.Copy, scale=float(D) ** -0.5).then_inc(M_ready, 1)
            nc.scalar.activation(crow[:, :], bank[1][0:1, KC * NSET:(KC + 1) * NSET], ACT.Copy, scale=float(D) ** -0.5).then_inc(M_ready, 1)
            def pair(i):
                for p in range(2):
                    a.wait_ge(hT_done[p], i + 1)
                    a.wait_ge(sc_done[p], i)
                    nc.scalar.activation(hT[p][:, :, :].rearrange("p k t -> p (k t)"), bank[2 + p][:, :], ACT.Copy).then_inc(hT_ready[p], 1)

            pair(0)
            with a.Fori(1, NT // 2) as i:
                pair(i)
            a.wait_ge(vs, 1)
            nc.scalar.activation(eg[:, :], gap[:, :], ACT.Exp).then_inc(eg_ready, 1)
            for t in range(NT):
                p, i = t % 2, t // 2
                a.wait_ge(wT_done[p], i + 1)
                if i:
                    a.wait_ge(o_done[p], i)
                nc.scalar.activation(wT[p][:, :], bank[6 + p][0:NSET, 0:P], ACT.Copy).then_inc(wT_ready[p], 1)

        @block.vector
        def _(v):
            for t in range(NT):
                if t:
                    v.wait_ge(stat, 2 * t)
                nc.vector.bn_stats(stats[:, :], x_sb[:, t, :]).then_inc(stat, 1)
                v.wait_ge(stat, 2 * t + 1)
                nc.vector.bn_aggr(mv[:, t, :], stats[:, :]).then_inc(stat, 1)
            v.wait_ge(par_in, 80)
            nc.vector.tensor_copy(itf[:, :, :], itok[:, :, :]).then_inc(bias_ready, 1)
            for c in range(CH):
                for k in range(TOPK_IN):
                    v.wait_ge(bias_ready, 1 + c * 5 + k)
                    if k == 0:
                        nc.vector.tensor_scalar(bias[:, c, :], iota, itf[:, c, 0:1], None, ALU.is_equal).then_inc(bias_ready, 1)
                    else:
                        nc.vector.scalar_tensor_tensor(out=bias[:, c, :], in0=iota, scalar=itf[:, c, k:k + 1], in1=bias[:, c, :],
                                                       op0=ALU.is_equal, op1=ALU.max).then_inc(bias_ready, 1)
                v.wait_ge(bias_ready, 1 + c * 5 + 4)
                nc.vector.tensor_scalar(bias[:, c, :], bias[:, c, :], 1e30, -1e30, ALU.mult, ALU.add).then_inc(bias_ready, 1)
            v.wait_ge(small, 4)
            v.wait_ge(stat, 2 * NT)
            v.wait_ge(bias_ready, 1 + 5 * CH)
            def norm(i):
                for p in range(2):
                    if not isinstance(i, int) or i:
                        v.wait_ge(hT_done[p], i)
                    nc.vector.tensor_scalar(hn[p][:, :], x_sb[:, ds(i * 2 + p, 1), :].squeeze(1), mv[:, ds(i * 2 + p, 1), 0],
                                            rstd[:, ds(i * 2 + p, 1)], ALU.subtract, ALU.mult).then_inc(hn_ready[p], 1)

            def keep_scores(i):
                for p in range(2):
                    v.wait_ge(sc_done[p], i + 1)
                    nc.vector.tensor_copy(score[:, ds(i * 2 + p, 1), :].squeeze(1), bank[4 + p][:, 0:NSET]).then_inc(score_ready[p], 1)

            overlapped_pairs(v, norm, keep_scores)
            for p in range(2):
                v.wait_ge(score_ready[p], NT // 2)
            nc.vector.tensor_tensor(score[:, :, :].rearrange("p (b c) n -> p b (c n)", b=B), score[:, :, :].rearrange("p (b c) n -> p b (c n)", b=B),
                                    over(bias[:, :, :].rearrange("p c n -> p (c n)"), 1, B), ALU.add).then_inc(vlink, 1)
            v.wait_ge(vlink, 1)
            link = chain(v, vlink, 1)
            link(nc.vector.memset(den[:, :], 0.0))
            for t in range(NT):
                nc.vector.max(top[:, t, :], score[:, t, :]).then_inc(tops, 1)
            for t in range(NT):
                v.wait_ge(tops, t + 1)
                nc.vector.max_index(topi[:, t, :], top[:, t, :], score[:, t, :]).then_inc(tops, 1)
            v.wait_ge(tops, 2 * NT)
            link(nc.vector.tensor_copy(idx[:, :, :], topi[:, :, 0:2]))
            nc.vector.tensor_tensor(gap[:, :], top[:, :, 1], top[:, :, 0], ALU.subtract).then_inc(vs, 1)
            v.wait_ge(eg_ready, 1)
            link(nc.vector.tensor_scalar(den[:, :], eg[:, :], 1.0, None, ALU.add))
            link(nc.vector.reciprocal(w0[:, :], den[:, :]))
            link(nc.vector.tensor_tensor(w1[:, :], eg[:, :], w0[:, :], ALU.mult))
            for w, k, wk in ((wt, 0, w0), (wt1, 1, w1)):
                link(nc.vector.tensor_tensor(w[:, :, :], over(iota, 1, NT), over(idx[:, :, k], 2, NSET), ALU.is_equal))
                link(nc.vector.tensor_tensor(w[:, :, :], w[:, :, :], over(wk[:, :], 2, NSET), ALU.mult))
            nc.vector.tensor_tensor(wt[:, :, :], wt[:, :, :], wt1[:, :, :], ALU.add).then_inc(wt_ready, 1)
            for t in range(NT):
                p, i = t % 2, t // 2
                v.wait_ge(o_done[p], i + 1)
                nc.vector.tensor_tensor(x_sb[:, t, :], x_sb[:, t, :], bank[p][:, :], ALU.add).then_inc(added[p], 1)
                v.wait_ge(added[p], i + 1)
                v.wait_ge(stat, 2 * (NT + t))
                nc.vector.bn_stats(stats[:, :], x_sb[:, t, :]).then_inc(stat, 1)
                v.wait_ge(stat, 2 * (NT + t) + 1)
                nc.vector.bn_aggr(ffn_mv[:, t, :], stats[:, :]).then_inc(stat, 1)


def chain(eng, sem, start=0):
    count = [start]

    def link(ins):
        count[0] += 1
        ins.then_inc(sem, 1)
        eng.wait_ge(sem, count[0])

    return link


def stage_ffn(nc, io, keep):
    x_sb, cst, bank, st, st_in, mv = (keep[k] for k in ("x", "cst", "bank", "st", "st_in", "ffn_mv"))
    NH, FB = FF // P, FF // 512
    with ExitStack() as ctx:
        def sb(name, shape, dt=F32):
            return ctx.enter_context(nc.sbuf_tensor("f_" + name, shape, dt))

        def sem(name):
            return ctx.enter_context(nc.semaphore("f_" + name))

        rnd = [sb(f"rnd{q}", [P, NQ, D]) for q in range(2)]
        tern = [sb(f"tern{q}", [P, NQ, D], BF16) for q in range(2)]
        wgT = sb("wgT", [P, KC, FF], BF16)
        wvT = sb("wvT", [P, KC, FF], BF16)
        woT = sb("woT", [P, NH, D], BF16)
        idb = sb("idb", [P, P], BF16)
        onesm = sb("onesm", [P, P])
        asum = sb("asum", [P, 3, NQ])
        asum1 = sb("asum1", [P, 3])
        gam = sb("gam", [P, 3])
        rgam = sb("rgam", [P, 3])
        gb = sb("gb", [P, FF])
        vb = sb("vb", [P, FF])
        ob = sb("ob", [P, D])
        var = sb("var", [P, NT])
        half = sb("half", [P, NT])
        rstd = sb("rstd", [P, NT])
        hn = sb("hn", [P, D])
        hr = sb("hr", [P, D])
        hq = sb("hq", [P, D], BF16)
        hqT = [sb(f"hqT{p}", [P, KC, P], BF16) for p in range(2)]
        g4 = sb("g4", [P, 4])
        fs = [sb(f"fs{p}", [P, 2]) for p in range(2)]
        zg = [st[p][:, :, :].rearrange("p k d -> p (k d)") for p in range(2)]
        zv = [st[2 + p][:, :, :].rearrange("p k d -> p (k d)") for p in range(2)]
        aq = tern[0][:, :, :].rearrange("p k d -> p (k d)")
        aqT = tern[1][:, :, :].rearrange("p k d -> p (k d)").rearrange("p (k t) -> p k t", k=NH)
        a4 = sb("a4", [P, 4])
        fo = [sb(f"fo{p}", [P, 1]) for p in range(2)]
        outt = [sb(f"outt{p}", [P, D]) for p in range(2)]

        names = """par_in gsmall asum_ready gsum_done gam_ready vw rnd_ready clip_ready tern_ready wT_done wT_ready
            hq_ready hqT_done hqT_ready gate_done val_done zg_ready silu_ready zv_ready prod_ready scale_ready round_ready
            aq_ready aqT_done aqT_ready xo_ready link_h link_a fs_ready fo_ready out_done out_ready""".split()
        s = {name: sem(name) for name in names}
        stored = [sem(f"stored{p}") for p in range(2)]
        block = ctx.enter_context(nc.Block())

        def past(eng, sem, value, held=None):
            if not isinstance(value, int) or value > 0:
                eng.wait_ge(sem, value)
                if held is not None and not isinstance(value, int):
                    eng.sem_inc(held, 1)

        def slots(eng, body):
            for u in range(2):
                body(u, u, True, True, u > 0, False)
            with eng.Fori(1, NT // 2 - 1) as i:
                for p in range(2):
                    body(i * 2 + p, p, True, True, True, True)
            for u in range(NT - 2, NT + 2):
                body(u, u % 2, u < NT, u + 1 < NT, u < NT + 1, True)

        @block.sync
        def _(sp):
            for w in range(1, 3):
                for q in range(NQ):
                    sp.wait_ge(s["rnd_ready"], (w - 1) * NQ + q + 1)
                    sp.dma_start(st[q][:, :, :], weight_quarter(io, w, q)).then_inc(st_in[q], 16)
                if w == 1:
                    sp.dma_start(gb[:, :], io["L0_ffn_gate_b"].partition_broadcast(P)).then_inc(s["par_in"], 16)
                    sp.dma_start(vb[:, :], io["L0_ffn_val_b"].partition_broadcast(P)).then_inc(s["par_in"], 16)
                    sp.dma_start(ob[:, :], io["L0_ffn_out_b"].partition_broadcast(P)).then_inc(s["par_in"], 16)

            def store(u, p, now, nxt, last, before):
                if before:
                    sp.wait_ge(s["out_ready"], u - 1)
                    sp.dma_start(io["out"].rearrange("b t d -> (b t) d")[ds((u - 2) * P, P), :], outt[p][:, :]).then_inc(stored[p], 16)

            slots(sp, store)
            for p in range(2):
                sp.wait_ge(stored[p], 16 * (NT // 2))

        @block.gpsimd
        def _(pool):
            nc.gpsimd.memset(half[:, :], -0.5).then_inc(s["gsmall"], 1)
            nc.gpsimd.memset(onesm[:, :], 1.0 / (FF * D)).then_inc(s["gsmall"], 1)
            nc.gpsimd.tensor_copy(idb[:, :], cst[:, C_ID:C_ID + P]).then_inc(s["gsmall"], 1)
            nc.gpsimd.tensor_scalar(var[:, :], mv[:, :, 1], LN_EPS, None, ALU.add).then_inc(s["gsmall"], 1)
            pool.wait_ge(s["gsmall"], 4)
            nc.gpsimd.tensor_tensor(rstd[:, :], var[:, :], half[:, :], ALU.pow).then_inc(s["gsmall"], 1)
            pool.wait_ge(s["par_in"], 48)

            def slot(u, p, now, nxt, last, before):
                if now:
                    for f in range(FB):
                        fsl = slice(f * 512, (f + 1) * 512)
                        past(pool, s["zv_ready"], u * FB + f + 1)
                        past(pool, s["silu_ready"], u * FB + f + 1, keep["held"][str(pool.engine)])
                        nc.gpsimd.tensor_tensor(zv[p][:, fsl], zv[p][:, fsl], zg[p][:, fsl], ALU.mult).then_inc(s["prod_ready"], 1)
                if last:
                    past(pool, stored[1 - p], 16 * ((u - 1 - (1 - p)) // 2) if isinstance(u, int) else ((u - p) * 8 - 16 * (1 - p)),
                         keep["held"][str(pool.engine)])
                    nc.gpsimd.tensor_tensor(outt[1 - p][:, :], x_sb[:, ds(u - 1, 1), :].squeeze(1), ob[:, :], ALU.add).then_inc(s["xo_ready"], 1)

            slots(pool, slot)

        @block.scalar
        def _(a):
            def evacuate(e):
                w, q = divmod(e, NQ)
                for k in range(NQ):
                    a.wait_ge(s["wT_done"], e * NQ + k + 1)
                    pt = bank[2 + k][:, :].bitcast(BF16)[:, 0:D].rearrange("p (k t) -> p k t", k=KC)
                    if w < 2:
                        dst = (wgT, wvT)[w][:, :, (q * NQ + k) * P:(q * NQ + k + 1) * P]
                    else:
                        dst = woT[:, q * NQ:(q + 1) * NQ, k * P:(k + 1) * P]
                    nc.scalar.activation(dst, pt, ACT.Copy).then_inc(s["wT_ready"], 1)

            for e in range(3 * NQ):
                w, q = divmod(e, NQ)
                if q == 0:
                    a.wait_ge(s["gam_ready"], w + 1)
                if e >= 2:
                    a.wait_ge(s["tern_ready"], e - 1)
                nc.scalar.activation(rnd[e % 2][:, :, :], st[q][:, :, :], ACT.Copy, scale=rgam[:, w:w + 1], bias=ROUND).then_inc(s["rnd_ready"], 1)
                if e:
                    evacuate(e - 1)
            evacuate(3 * NQ - 1)

            def turned_h(t, p):
                past(a, s["hqT_done"], t + 1)
                nc.scalar.activation(hqT[p][:, :, :].rearrange("p k t -> p (k t)"), bank[7][:, :].bitcast(BF16)[:, 0:D], ACT.Copy)\
                    .then_inc(s["hqT_ready"], 1)

            turned_h(0, 0)

            def slot(u, p, now, nxt, last, before):
                for f in range(FB):
                    fsl = slice(f * 512, (f + 1) * 512)
                    if now:
                        past(a, s["zg_ready"], u * FB + f + 1)
                        nc.scalar.activation(zg[p][:, fsl], zg[p][:, fsl], ACT.Silu).then_inc(s["silu_ready"], 1)
                    if f == 0 and last:
                        past(a, s["scale_ready"], u, keep["held"][str(a.engine)])
                        nc.scalar.activation(zg[1 - p], zv[1 - p], ACT.Copy, scale=a4[:, 2:3], bias=ROUND).then_inc(s["round_ready"], 1)
                if nxt:
                    turned_h(u + 1, 1 - p)
                if last:
                    past(a, s["out_done"], u - 1)
                    for h in range(2):
                        past(a, s["aqT_done"], u * 2 - 1 + h)
                        nc.scalar.activation(aqT[:, h * 8:(h + 1) * 8, :].rearrange("p k t -> p (k t)"), bank[(6, 4)[h]][:, :].bitcast(BF16),
                                             ACT.Copy).then_inc(s["aqT_ready"], 1)

            slots(a, slot)

        @block.tensor
        def _(pe):
            pe.wait_ge(s["gsmall"], 3)
            for w in range(3):
                for q in range(NQ):
                    e = w * NQ + q
                    if q == 0 and w == 0:
                        pe.wait_ge(s["asum_ready"], 1)
                        nc.tensor.matmul(bank[0][:, 0:1], onesm[:, :], asum1[:, 0:1], start=True, stop=True).then_inc(s["gsum_done"], 1)
                    pe.wait_ge(s["tern_ready"], e + 1)
                    for k in range(NQ):
                        if e:
                            pe.wait_ge(s["wT_ready"], (e - 1) * NQ + k + 1)
                        for d in range(KC):
                            last = nc.tensor.transpose(bank[2 + k][:, :].bitcast(BF16)[:, d * P:(d + 1) * P], tern[e % 2][:, k, d * P:(d + 1) * P], idb[:, :])
                        last.then_inc(s["wT_done"], 1)
                    if q == NQ - 1 and w < 2:
                        pe.wait_ge(s["asum_ready"], w + 2)
                        nc.tensor.matmul(bank[0][:, w + 1:w + 2], onesm[:, :], asum1[:, w + 1:w + 2], start=True, stop=True).then_inc(s["gsum_done"], 1)

            def turn_h(t):
                past(pe, s["hq_ready"], t + 1)
                past(pe, s["hqT_ready"], t)
                for k in range(KC):
                    last = nc.tensor.transpose(bank[7][:, :].bitcast(BF16)[:, k * P:(k + 1) * P], hq[:, k * P:(k + 1) * P], idb[:, :])
                last.then_inc(s["hqT_done"], 1)

            turn_h(0)
            pe.wait_ge(s["wT_ready"], 3 * NQ * NQ)

            def slot(u, p, now, nxt, last, before):
                for f in range(FB):
                    if now:
                        if f == 0:
                            past(pe, s["hqT_ready"], u + 1)
                        fsl = slice(f * 512, (f + 1) * 512)
                        for wT, b0, done, read in ((wgT, 0, "gate_done", "zg_ready"), (wvT, 2, "val_done", "zv_ready")):
                            past(pe, s[read], u * FB + f - 1)
                            for k in range(KC):
                                ins = nc.tensor.matmul(bank[b0 + f % 2][:, :], hqT[p][:, k, :], wT[:, k, fsl], start=(k == 0), stop=(k == KC - 1))
                            ins.then_inc(s[done], 1)
                    if f == 1 and before:
                        past(pe, s["aqT_ready"], u * 2 - 2)
                        past(pe, s["out_ready"], u - 2)
                        for k in range(NH):
                            ins = nc.tensor.matmul(bank[5][:, :], aqT[:, k, :], woT[:, k, :], start=(k == 0), stop=(k == NH - 1))
                        ins.then_inc(s["out_done"], 1)
                if nxt:
                    turn_h(u + 1)
                if last:
                    past(pe, s["aq_ready"], u)
                    past(pe, s["aqT_ready"], u * 2 - 2)
                    for h in range(2):
                        for k in range(8):
                            ins = nc.tensor.transpose(bank[(6, 4)[h]][:, :].bitcast(BF16)[:, k * P:(k + 1) * P],
                                                      aq[:, (h * 8 + k) * P:(h * 8 + k + 1) * P], idb[:, :])
                        ins.then_inc(s["aqT_done"], 1)

            slots(pe, slot)

        @block.vector
        def _(v):
            def abs_sum(w, q):
                v.wait_ge(st_in[q], 16 * (w + 1))
                nc.vector.tensor_reduce(asum[:, w, q:q + 1], st[q][:, :, :].rearrange("p k d -> p (k d)"), AXX, ALU.add,
                                        apply_absolute_value=True).then_inc(s["vw"], 1)

            def total(w):
                v.wait_ge(s["vw"], 5 * w + 4)
                nc.vector.tensor_reduce(asum1[:, w:w + 1], asum[:, w, :], AXX, ALU.add).then_inc(s["asum_ready"], 1)

            def scale(w):
                v.wait_ge(s["gsum_done"], w + 1)
                nc.vector.tensor_scalar(gam[:, w:w + 1], bank[0][:, w:w + 1], 1e-5, None, ALU.max).then_inc(s["vw"], 1)
                v.wait_ge(s["vw"], 5 * w + 5)
                nc.vector.reciprocal(rgam[:, w:w + 1], gam[:, w:w + 1]).then_inc(s["gam_ready"], 1)

            for q in range(NQ):
                abs_sum(0, q)
            total(0)
            scale(0)
            for w in range(3):
                for q in range(NQ):
                    e = w * NQ + q
                    r = rnd[e % 2]
                    v.wait_ge(s["rnd_ready"], e + 1)
                    nc.vector.tensor_scalar(r[:, :, :], r[:, :, :], ROUND, 1.0, ALU.subtract, ALU.min).then_inc(s["clip_ready"], 1)
                    v.wait_ge(s["clip_ready"], e + 1)
                    if e >= 2:
                        v.wait_ge(s["wT_done"], (e - 1) * NQ)
                    nc.vector.tensor_scalar(tern[e % 2][:, :, :], r[:, :, :], -1.0, None, ALU.max).then_inc(s["tern_ready"], 1)
                    if w < 2 and q:
                        abs_sum(w + 1, q - 1)
                if w < 2:
                    abs_sum(w + 1, NQ - 1)
                    total(w + 1)
                    scale(w + 1)
            v.wait_ge(s["gsmall"], 5)
            v.wait_ge(s["gam_ready"], 3)
            v.wait_ge(s["par_in"], 48)
            v.wait_ge(s["wT_done"], 3 * NQ * NQ)

            def norm(t, p):
                count = [0]

                def link(ins):
                    count[0] += 1
                    ins.then_inc(s["link_h"], 1)
                    v.wait_ge(s["link_h"], t * 6 + count[0])

                link(nc.vector.tensor_scalar(hn[:, :], x_sb[:, ds(t, 1), :].squeeze(1), mv[:, ds(t, 1), 0], rstd[:, ds(t, 1)],
                                             ALU.subtract, ALU.mult))
                link(nc.vector.tensor_reduce(g4[:, 0:1], hn[:, :], AXX, ALU.max, apply_absolute_value=True))
                link(nc.vector.tensor_scalar(g4[:, 0:1], g4[:, 0:1], 1e-5, None, ALU.max))
                link(nc.vector.reciprocal(g4[:, 1:2], g4[:, 0:1]))
                link(nc.vector.tensor_scalar(g4[:, 2:3], g4[:, 1:2], 127.0, None, ALU.mult))
                past(v, s["hq_ready"], t)
                link(nc.vector.tensor_scalar(hr[:, :], hn[:, :], g4[:, 2:3], ROUND, ALU.mult, ALU.add))
                past(v, s["hqT_done"], t)
                nc.vector.tensor_scalar(hq[:, :], hr[:, :], ROUND, 127.0, ALU.subtract, ALU.min).then_inc(s["hq_ready"], 1)
                past(v, s["zv_ready"], (t - 1) * FB)
                for w in range(2):
                    nc.vector.tensor_scalar(fs[p][:, w:w + 1], g4[:, 0:1], gam[:, w:w + 1], 1.0 / 127.0, ALU.mult, ALU.mult)\
                        .then_inc(s["fs_ready"], 1)

            norm(0, 0)

            def slot(u, p, now, nxt, last, before):
                def hidden(f):
                    fsl = slice(f * 512, (f + 1) * 512)
                    if f == 0:
                        past(v, s["fs_ready"], u * 2 + 2)
                        past(v, s["aq_ready"], u - 1)
                        past(v, s["round_ready"], u - 1)
                    past(v, s["gate_done"], u * FB + f + 1)
                    nc.vector.scalar_tensor_tensor(out=zg[p][:, fsl], in0=bank[f % 2][:, :], scalar=fs[p][:, 0:1], in1=gb[:, fsl],
                                                   op0=ALU.mult, op1=ALU.add).then_inc(s["zg_ready"], 1)
                    past(v, s["val_done"], u * FB + f + 1)
                    nc.vector.scalar_tensor_tensor(out=zv[p][:, fsl], in0=bank[2 + f % 2][:, :], scalar=fs[p][:, 1:2], in1=vb[:, fsl],
                                                   op0=ALU.mult, op1=ALU.add).then_inc(s["zv_ready"], 1)

                def act_scale():
                    t = u - 1

                    def link(ins, k):
                        ins.then_inc(s["link_a"], 1)
                        v.wait_ge(s["link_a"], t * 3 + k)

                    past(v, s["prod_ready"], u * FB)
                    past(v, s["round_ready"], t)
                    past(v, s["fo_ready"], t)
                    link(nc.vector.tensor_reduce(a4[:, 0:1], zv[1 - p], AXX, ALU.max, apply_absolute_value=True), 1)
                    link(nc.vector.tensor_scalar(a4[:, 0:1], a4[:, 0:1], 1e-5, None, ALU.max), 2)
                    link(nc.vector.reciprocal(a4[:, 1:2], a4[:, 0:1]), 3)
                    nc.vector.tensor_scalar(a4[:, 2:3], a4[:, 1:2], 127.0, None, ALU.mult).then_inc(s["scale_ready"], 1)
                    past(v, s["out_ready"], t - 1)
                    nc.vector.tensor_scalar(fo[1 - p][:, :], a4[:, 0:1], gam[:, 2:3], 1.0 / 127.0, ALU.mult, ALU.mult).then_inc(s["fo_ready"], 1)

                if now:
                    hidden(0)
                if last:
                    act_scale()
                if now:
                    hidden(1)
                if nxt:
                    norm(u + 1, 1 - p)
                if now:
                    hidden(2)
                if last:
                    past(v, s["round_ready"], u)
                    past(v, s["aqT_done"], u * 2 - 2)
                    nc.vector.tensor_scalar(aq, zg[1 - p], ROUND, 127.0, ALU.subtract, ALU.min).then_inc(s["aq_ready"], 1)
                if now:
                    hidden(3)
                if before:
                    past(v, s["out_done"], u - 1)
                    past(v, s["xo_ready"], u - 1)
                    past(v, s["fo_ready"], u - 1)
                    nc.vector.scalar_tensor_tensor(out=outt[p][:, :], in0=bank[5][:, :], scalar=fo[p][:, 0:1], in1=outt[p][:, :],
                                                   op0=ALU.mult, op1=ALU.add).then_inc(s["out_ready"], 1)

            slots(v, slot)


def build(nc, io):
    with ExitStack() as ctx:
        keep = {
            "x": ctx.enter_context(nc.sbuf_tensor("x", [P, NT, D], F32)),
            "cst": ctx.enter_context(nc.sbuf_tensor("cst", [P, C_ALL], F32)),
            "bank": [ctx.enter_context(nc.psum_tensor(f"bank{i}", [P, 512], F32)) for i in range(8)],
        }
        keep["held"] = {str(e.engine): ctx.enter_context(nc.semaphore(name + "_held"))
                        for name, e in (("pe", nc.tensor), ("act", nc.scalar), ("pool", nc.gpsimd), ("sp", nc.sync))}
        with ExitStack() as attn:
            keep["hhi"] = attn.enter_context(nc.sbuf_tensor("hhi", [P, KC, B * T], F16))
            keep["hlo"] = attn.enter_context(nc.sbuf_tensor("hlo", [P, KC, B * T], F16))
            keep["sc"] = attn.enter_context(nc.sbuf_tensor("sc", [P, 5, NS, B], F32))
            keep["dec"] = attn.enter_context(nc.sbuf_tensor("dec", [P, NS, B], F32))
            stage_norm_and_scalars(nc, io, keep)
            stage_delta_rule(nc, io, keep)
        keep["st"] = [ctx.enter_context(nc.sbuf_tensor(f"st{q}", [P, NQ, D], F32)) for q in range(NQ)]
        keep["st_in"] = [ctx.enter_context(nc.semaphore(f"st_in{q}")) for q in range(NQ)]
        keep["ffn_mv"] = ctx.enter_context(nc.sbuf_tensor("ffn_mv", [P, NT, 2], F32))
        stage_sets(nc, io, keep)
        stage_ffn(nc, io, keep)


_INS = ["x", "ctx_2048", "itok_Sx4_0_63", "L0_attn_Wq", "L0_attn_Wk", "L0_attn_Wv", "L0_attn_conv_q", "L0_attn_conv_k",
        "L0_attn_conv_v", "L0_attn_Wb", "L0_attn_Wa", "L0_attn_A_log", "L0_attn_dt_bias", "L0_attn_Wg", "L0_attn_norm_weight",
        "L0_attn_Wo", "L0_xattn_desc_router", "L0_xattn_W_q", "L0_xattn_b_q", "L0_ffn_gate_w", "L0_ffn_gate_b", "L0_ffn_val_w",
        "L0_ffn_val_b", "L0_ffn_out_w", "L0_ffn_out_b"]


def kernel(**inputs):
    import numpy as _np
    import concourse.bacc as _bacc
    from concourse import mybir as _mybir
    from concourse.bass_utils import run_bass_kernel_spmd as _run

    nc = _bacc.Bacc("TRN2", target_bir_lowering=False, num_devices=1)
    arrays, io = {}, {}
    for name in _INS:
        a = _np.ascontiguousarray(inputs[name])
        arrays[f"in_{name}_dram"] = a
        io[name] = nc.dram_tensor(f"in_{name}_dram", a.shape, _mybir.dt.from_np(a.dtype), kind="ExternalInput").ap()
    arrays["shape_constants"] = shape_constants()
    io["cst"] = nc.dram_tensor("shape_constants", arrays["shape_constants"].shape, _mybir.dt.float32, kind="ExternalInput").ap()
    io["out"] = nc.dram_tensor("out_0_dram", (B, T, D), _mybir.dt.float32, kind="ExternalOutput").ap()
    build(nc, io)
    r = _run(nc, [arrays], core_ids=[0])
    return r.results[0]["out_0_dram"]
```
